# Optimizing a Trainium2 kernel written in Bass

```python
import numpy as np
import jax
import jax.numpy as jnp

def _softmax(x, axis=-1):
    return jax.nn.softmax(x, axis=axis)

def _gelu(x):
    return jax.nn.gelu(x, approximate=True)

def _silu(x):
    return jax.nn.silu(x)

def _sigmoid(x):
    return jax.nn.sigmoid(x)

def _layernorm(x, axis=-1, eps=1e-05):
    m = jnp.mean(x, axis=axis, keepdims=True)
    v = jnp.var(x, axis=axis, keepdims=True)
    return (x - m) / jnp.sqrt(v + eps)

def _scatter_add(tgt, idx, src, axis=0):
    return tgt.at[idx].add(src)

def _segment_sum(src, seg, n):
    return jax.ops.segment_sum(src, seg, n)
kernel_name = 'mk_xattn_ffn_d2_seqx_r8_659a2a'

def setup_inputs(seed: int=0):
    np.random.seed(seed)
    _w = jnp.asarray

    def _rec_inputs():
        import jax
        import jax.numpy as jnp
        _rk = jax.random.key(seed)
        x = 7.22e-05 + 1 * jax.random.normal(jax.random.fold_in(_rk, 1), (16, 56, 256), jnp.float32)
        _lenS = 56 - jax.random.randint(jax.random.fold_in(_rk, 7), (16,), 0, max(1, 56 // 4) + 1, jnp.int32)
        _lenS2 = 1500 - jax.random.randint(jax.random.fold_in(_rk, 8), (16,), 0, max(1, 1500 // 4) + 1, jnp.int32)
        _ctx_2048P = jax.random.normal(jax.random.fold_in(_rk, 11), (16, 16, 256), jnp.float32)
        _ctx_2048c = jax.random.dirichlet(jax.random.fold_in(_rk, 511), 0.3 * jnp.ones((16,), jnp.float32), (16, 1500))
        _ctx_2048t = jnp.einsum('bsk,bkd->bsd', _ctx_2048c, _ctx_2048P)
        _ctx_2048t = _ctx_2048t * jax.lax.rsqrt(jnp.mean(jnp.square(_ctx_2048t)) + 1e-12) * 0.953939
        ctx_2048 = -0.000514642 + 1.00011 * (_ctx_2048t + 0.3 * jax.random.normal(jax.random.fold_in(_rk, 611), (16, 1500, 256), jnp.float32))
        return (x, ctx_2048)
    x, ctx_2048 = _rec_inputs()

    def _L0_xattn_setup():
        import jax, jax.numpy as jnp
        import numpy as np
        D_MODEL = 256
        NUM_HEADS = 16
        HEAD_DIM = D_MODEL // NUM_HEADS

        def _fq_sym(x, axis):
            s = jnp.max(jnp.abs(x), axis=axis, keepdims=True) / 127.0
            s = jnp.maximum(s, 1e-08)
            q = jnp.clip(jnp.round(x / s), -127.0, 127.0) * s
            return x + jax.lax.stop_gradient(q - x)

        def _fq_unsigned(x, axis):
            s = jnp.max(x, axis=axis, keepdims=True) / 255.0
            s = jnp.maximum(s, 1e-08)
            q = jnp.clip(jnp.round(x / s), 0.0, 255.0) * s
            return x + jax.lax.stop_gradient(q - x)
        key = jax.random.key(seed)
        ks = jax.random.split(key, 8)
        B, N, M, C = (2, 256, 64, D_MODEL)
        return {'x': jax.random.normal(ks[0], (B, N, C), jnp.float32), 'cond': jax.random.normal(ks[1], (B, M, C), jnp.float32), 'Wq': jax.random.normal(ks[2], (C, C), jnp.float32) * 0.02, 'bq': jnp.zeros((C,), jnp.float32), 'Wkv': jax.random.normal(ks[3], (C, 2 * C), jnp.float32) * 0.02, 'bkv': jnp.zeros((2 * C,), jnp.float32), 'Wp': jax.random.normal(ks[4], (C, C), jnp.float32) * 0.02, 'bp': jnp.zeros((C,), jnp.float32)}
    _L0_xattn_all = _L0_xattn_setup()
    _L0_xattn_in = {k: v for k, v in _L0_xattn_all.items() if k in ('Wq', 'bq', 'Wkv', 'bkv', 'Wp', 'bp')}
    del _L0_xattn_all

    def _L0_ffn_setup():
        import jax, jax.numpy as jnp
        import numpy as np
        HID = 256
        N_EXP = 32
        F_EXP = 96
        TOP_K = 6
        F_SH = 192
        B, S = (1, 128)
        key = jax.random.key(seed)
        ks = jax.random.split(key, 8)
        s = 0.02
        return {'hidden_states': jax.random.normal(ks[0], (B, S, HID), dtype=jnp.float32), 'gate_w': jax.random.normal(ks[1], (HID, N_EXP), dtype=jnp.float32) * s, 'wg': jax.random.normal(ks[2], (N_EXP, HID, F_EXP), dtype=jnp.float32) * s, 'wu': jax.random.normal(ks[3], (N_EXP, HID, F_EXP), dtype=jnp.float32) * s, 'wd': jax.random.normal(ks[4], (N_EXP, F_EXP, HID), dtype=jnp.float32) * s, 'sg': jax.random.normal(ks[5], (HID, F_SH), dtype=jnp.float32) * s, 'su': jax.random.normal(ks[6], (HID, F_SH), dtype=jnp.float32) * s, 'sd': jax.random.normal(ks[7], (F_SH, HID), dtype=jnp.float32) * s}
    _L0_ffn_all = _L0_ffn_setup()
    _L0_ffn_in = {k: v for k, v in _L0_ffn_all.items() if k in ('gate_w', 'wg', 'wu', 'wd', 'sg', 'su', 'sd')}
    del _L0_ffn_all

    def _L1_xattn_setup():
        import jax, jax.numpy as jnp
        import numpy as np
        from jax import lax
        LN_EPS = 1e-05
        key = jax.random.key(seed)
        ks = jax.random.split(key, 8)
        B, S, T, D = (4, 128, 256, 256)
        scale = 0.02
        return {'Z': jax.random.normal(ks[0], (B, S, D), dtype=jnp.float32), 'kv': jax.random.normal(ks[1], (B, T, D), dtype=jnp.float32), 'decay': jnp.float32(0.9), 'W_in': jax.random.normal(ks[2], (D, D), dtype=jnp.float32) * scale, 'b_in': jnp.zeros((D,), dtype=jnp.float32), 'W_out': jax.random.normal(ks[3], (D, D), dtype=jnp.float32) * scale, 'b_out': jnp.zeros((D,), dtype=jnp.float32), 'gamma': jnp.ones((D,), dtype=jnp.float32), 'beta': jnp.zeros((D,), dtype=jnp.float32)}
    _L1_xattn_all = _L1_xattn_setup()
    _L1_xattn_in = {k: v for k, v in _L1_xattn_all.items() if k in ('decay', 'W_in', 'b_in', 'W_out', 'b_out', 'gamma', 'beta')}
    del _L1_xattn_all

    def _L1_ffn_setup():
        import jax, jax.numpy as jnp
        import numpy as np
        H = 256
        I = 176
        E = 8
        K = 2
        B, S = (4, 256)

        def _moe(x, router_w, w1, w2):
            b, s, h = x.shape
            xf = x.reshape(-1, h)
            T = xf.shape[0]
            logits = xf @ router_w.T
            topk_vals, topk_idx = jax.lax.top_k(logits, K)
            topk_w = jax.nn.softmax(topk_vals, axis=-1)
            exp_id = topk_idx.reshape(-1)
            exp_w = topk_w.reshape(-1)
            order = jnp.argsort(exp_id)
            x_sorted = xf[order // K]
            counts = jnp.bincount(exp_id, length=E).astype(jnp.int32)
            y1 = jax.lax.ragged_dot(x_sorted, jnp.swapaxes(w1, 1, 2), counts)
            gate, up = jnp.split(y1, 2, axis=-1)
            y_act = jax.nn.silu(gate) * up
            y2 = jax.lax.ragged_dot(y_act, jnp.swapaxes(w2, 1, 2), counts)
            inv = jnp.argsort(order)
            y_pairs = y2[inv] * exp_w[:, None]
            y = y_pairs.reshape(T, K, h).sum(axis=1)
            return y.reshape(b, s, h)
        key = jax.random.key(seed)
        k1, k2, k3, k4 = jax.random.split(key, 4)
        x = jax.random.normal(k1, (B, S, H), dtype=jnp.float32)
        router_w = jax.random.normal(k2, (E, H), dtype=jnp.float32) * 0.02
        w1 = jax.random.normal(k3, (E, 2 * I, H), dtype=jnp.float32) * 0.02
        w2 = jax.random.normal(k4, (E, H, I), dtype=jnp.float32) * 0.02
        return {'x': x, 'router_w': router_w, 'w1': w1, 'w2': w2}
    _L1_ffn_all = _L1_ffn_setup()
    _L1_ffn_in = {k: v for k, v in _L1_ffn_all.items() if k in ('router_w', 'w1', 'w2')}
    del _L1_ffn_all
    return {'x': x, 'ctx_2048': ctx_2048, 'L0_xattn_Wq': _L0_xattn_in['Wq'], 'L0_xattn_bq': _L0_xattn_in['bq'], 'L0_xattn_Wkv': _L0_xattn_in['Wkv'], 'L0_xattn_bkv': _L0_xattn_in['bkv'], 'L0_xattn_Wp': _L0_xattn_in['Wp'], 'L0_xattn_bp': _L0_xattn_in['bp'], 'L0_ffn_gate_w': _L0_ffn_in['gate_w'], 'L0_ffn_wg': _L0_ffn_in['wg'], 'L0_ffn_wu': _L0_ffn_in['wu'], 'L0_ffn_wd': _L0_ffn_in['wd'], 'L0_ffn_sg': _L0_ffn_in['sg'], 'L0_ffn_su': _L0_ffn_in['su'], 'L0_ffn_sd': _L0_ffn_in['sd'], 'L1_xattn_decay': _L1_xattn_in['decay'], 'L1_xattn_W_in': _L1_xattn_in['W_in'], 'L1_xattn_b_in': _L1_xattn_in['b_in'], 'L1_xattn_W_out': _L1_xattn_in['W_out'], 'L1_xattn_b_out': _L1_xattn_in['b_out'], 'L1_xattn_gamma': _L1_xattn_in['gamma'], 'L1_xattn_beta': _L1_xattn_in['beta'], 'L1_ffn_router_w': _L1_ffn_in['router_w'], 'L1_ffn_w1': _L1_ffn_in['w1'], 'L1_ffn_w2': _L1_ffn_in['w2']}

def reference(x, ctx_2048, L0_xattn_Wq, L0_xattn_bq, L0_xattn_Wkv, L0_xattn_bkv, L0_xattn_Wp, L0_xattn_bp, L0_ffn_gate_w, L0_ffn_wg, L0_ffn_wu, L0_ffn_wd, L0_ffn_sg, L0_ffn_su, L0_ffn_sd, L1_xattn_decay, L1_xattn_W_in, L1_xattn_b_in, L1_xattn_W_out, L1_xattn_b_out, L1_xattn_gamma, L1_xattn_beta, L1_ffn_router_w, L1_ffn_w1, L1_ffn_w2):
    import jax
    import jax.numpy as jnp

    def _L0_xattn_ref(x, cond, Wq, bq, Wkv, bkv, Wp, bp):
        import jax, jax.numpy as jnp
        import numpy as np
        D_MODEL = 256
        NUM_HEADS = 16
        HEAD_DIM = D_MODEL // NUM_HEADS

        def _fq_sym(x, axis):
            s = jnp.max(jnp.abs(x), axis=axis, keepdims=True) / 127.0
            s = jnp.maximum(s, 1e-08)
            q = jnp.clip(jnp.round(x / s), -127.0, 127.0) * s
            return x + jax.lax.stop_gradient(q - x)

        def _fq_unsigned(x, axis):
            s = jnp.max(x, axis=axis, keepdims=True) / 255.0
            s = jnp.maximum(s, 1e-08)
            q = jnp.clip(jnp.round(x / s), 0.0, 255.0) * s
            return x + jax.lax.stop_gradient(q - x)
        B, N, C = x.shape
        H, hd = (NUM_HEADS, HEAD_DIM)
        q = (x @ Wq + bq).reshape(1, B * N, H, hd)
        kv = (cond @ Wkv + bkv).reshape(1, -1, 2, H, hd)
        k, v = (kv[:, :, 0], kv[:, :, 1])
        scale = 1.0 / np.sqrt(hd).astype(np.float32)
        q = jnp.transpose(q * scale, (0, 2, 1, 3))
        k = jnp.transpose(k, (0, 2, 1, 3))
        v = jnp.transpose(v, (0, 2, 1, 3))
        q = _fq_sym(q, axis=-1)
        k = _fq_sym(k, axis=-1)
        v = _fq_sym(v, axis=2)
        attn = jnp.einsum('bhqd,bhkd->bhqk', q, k)
        attn = jax.nn.softmax(attn.astype(jnp.float32), axis=-1)
        attn = _fq_unsigned(attn, axis=-1)
        out = jnp.einsum('bhqk,bhkd->bhqd', attn, v)
        out = jnp.transpose(out, (0, 2, 1, 3)).reshape(B, N, C)
        return out @ Wp + bp

    def _L0_ffn_ref(hidden_states, gate_w, wg, wu, wd, sg, su, sd):
        import jax, jax.numpy as jnp
        import numpy as np
        HID = 256
        N_EXP = 32
        F_EXP = 96
        TOP_K = 6
        F_SH = 192
        B, S = (1, 128)
        orig_shape = hidden_states.shape
        x = hidden_states.reshape(-1, HID)
        scores = jax.nn.sigmoid(x @ gate_w)
        topk_w, topk_i = jax.lax.top_k(scores, TOP_K)
        topk_w = topk_w / (jnp.sum(topk_w, axis=-1, keepdims=True) + 1e-20)
        combine = jnp.sum(jax.nn.one_hot(topk_i, N_EXP, dtype=topk_w.dtype) * topk_w[..., None], axis=1)
        g = jnp.einsum('td,edf->tef', x, wg)
        u = jnp.einsum('td,edf->tef', x, wu)
        act = jax.nn.silu(g) * u
        routed = jnp.einsum('tef,efd,te->td', act, wd, combine)
        routed = routed.reshape(orig_shape)
        shared = jax.nn.silu(hidden_states @ sg) * (hidden_states @ su) @ sd
        return routed + shared

    def _L1_xattn_ref(Z, kv, decay, W_in, b_in, W_out, b_out, gamma, beta):
        import jax, jax.numpy as jnp
        import numpy as np
        from jax import lax
        LN_EPS = 1e-05
        B, T, D = kv.shape
        K = jax.nn.sigmoid(decay)
        x = jnp.einsum('btd,ed->bte', kv, W_in) + b_in

        def scan_fn(s, xt):
            s = K * s + xt
            return (s, s)
        s0 = jnp.zeros((B, D), dtype=kv.dtype)
        _, states = lax.scan(scan_fn, s0, jnp.swapaxes(x, 0, 1))
        states = jnp.swapaxes(states, 0, 1)
        proj = jnp.einsum('btd,ed->bte', states, W_out) + b_out
        summary = jnp.mean(proj, axis=1, keepdims=True)
        y = Z + summary
        mu = jnp.mean(y, axis=-1, keepdims=True)
        var = jnp.mean((y - mu) ** 2, axis=-1, keepdims=True)
        return (y - mu) / jnp.sqrt(var + LN_EPS) * gamma + beta

    def _L1_ffn_ref(x, router_w, w1, w2):
        import jax, jax.numpy as jnp
        import numpy as np
        H = 256
        I = 176
        E = 8
        K = 2
        B, S = (4, 256)

        def _moe(x, router_w, w1, w2):
            b, s, h = x.shape
            xf = x.reshape(-1, h)
            T = xf.shape[0]
            logits = xf @ router_w.T
            topk_vals, topk_idx = jax.lax.top_k(logits, K)
            topk_w = jax.nn.softmax(topk_vals, axis=-1)
            exp_id = topk_idx.reshape(-1)
            exp_w = topk_w.reshape(-1)
            order = jnp.argsort(exp_id)
            x_sorted = xf[order // K]
            counts = jnp.bincount(exp_id, length=E).astype(jnp.int32)
            y1 = jax.lax.ragged_dot(x_sorted, jnp.swapaxes(w1, 1, 2), counts)
            gate, up = jnp.split(y1, 2, axis=-1)
            y_act = jax.nn.silu(gate) * up
            y2 = jax.lax.ragged_dot(y_act, jnp.swapaxes(w2, 1, 2), counts)
            inv = jnp.argsort(order)
            y_pairs = y2[inv] * exp_w[:, None]
            y = y_pairs.reshape(T, K, h).sum(axis=1)
            return y.reshape(b, s, h)
        return _moe(x, router_w, w1, w2)
    x = x + _L0_xattn_ref(_layernorm(x, axis=-1), ctx_2048, L0_xattn_Wq, L0_xattn_bq, L0_xattn_Wkv, L0_xattn_bkv, L0_xattn_Wp, L0_xattn_bp)
    x = x + _L0_ffn_ref(_layernorm(x, axis=-1), L0_ffn_gate_w, L0_ffn_wg, L0_ffn_wu, L0_ffn_wd, L0_ffn_sg, L0_ffn_su, L0_ffn_sd)
    x = x + _L1_xattn_ref(_layernorm(x, axis=-1), ctx_2048, L1_xattn_decay, L1_xattn_W_in, L1_xattn_b_in, L1_xattn_W_out, L1_xattn_b_out, L1_xattn_gamma, L1_xattn_beta)
    x = x + _L1_ffn_ref(_layernorm(x, axis=-1), L1_ffn_router_w, L1_ffn_w1, L1_ffn_w2)
    return x

_drawn_inputs = setup_inputs


def setup_inputs(seed=0):
    import zlib

    import numpy as np

    out = dict(_drawn_inputs(seed))
    spreads = {'L0_xattn_bq': (0.0, 0.8),
     'L0_xattn_bkv': (0.0, 0.1),
     'L0_xattn_bp': (0.0, 0.1),
     'L1_xattn_b_in': (0.0, 0.1),
     'L1_xattn_b_out': (0.0, 0.1),
     'L1_xattn_gamma': (1.0, 0.2),
     'L1_xattn_beta': (0.0, 0.1)}
    factors = {'L0_xattn_Wq': 8.0,
     'L0_xattn_Wkv': 4.404,
     'L0_ffn_gate_w': 8.0,
     'L0_ffn_wg': 8.0,
     'L0_ffn_wu': 8.0,
     'L0_ffn_wd': 8.0,
     'L0_ffn_sg': 3.97,
     'L0_ffn_su': 3.897,
     'L0_ffn_sd': 3.911,
     'L1_ffn_router_w': 8.0,
     'L1_ffn_w1': 8.0,
     'L1_ffn_w2': 8.0}
    for name, (base, spread) in spreads.items():
        noise = np.random.default_rng([zlib.crc32(name.encode()), seed]).standard_normal(out[name].shape)
        drawn = base * np.exp(spread * noise) if base else spread * noise
        out[name] = jnp.asarray(drawn.astype(out[name].dtype))
    for name, factor in factors.items():
        out[name] = (out[name] * factor).astype(out[name].dtype)
    return out
```

```python
import math
from contextlib import ExitStack

import concourse.bass as bass
from concourse import mybir

BATCH, SEQ, DIM = 16, 56, 256
TOK = BATCH * SEQ
LCTX = 1500
NKEY = BATCH * LCTX
HEADS, HDIM = 16, 16
P = 128
NC = DIM // P
TT = 2 * SEQ
NTT = TOK // TT
HALF = TOK // 2
TPH = HALF // TT
KT = 125
GEN = 4
NGEN = NKEY // (KT * GEN)
GK = KT * GEN
CT = 24
CK = CT * KT
NCH = NKEY // CK
QB = P
NQB = TOK // QB
SB = 500
NPIECE = CK // (2 * SB)
PARTS = 3
HROWS = PARTS * HDIM
KROWS = 2 * HROWS
MROWS = KROWS + PARTS
SUMROWS = 32
N_EXP0, N_SEL0, F0 = 32, 6, 96
N_ALL0 = N_EXP0 + 2
N_EXP1, N_SEL1, F1 = 8, 2, 88
N_ALL1 = 2 * N_EXP1
BANK = 512
ROUND = 12582912.0
QMAX = 127.0
EPS = 1e-5
LOG255 = math.log(255.0)
TINY = 1e-8


def build(nc, t):
    f32, bf16 = mybir.dt.float32, mybir.dt.bfloat16
    ALU, ACT, AX = mybir.AluOpType, mybir.ActivationFunctionType, mybir.AxisListType
    pe, act, dve, pool, sp = nc.tensor, nc.scalar, nc.vector, nc.gpsimd, nc.sync
    ctx = ExitStack()

    def semaphore(name):
        return ctx.enter_context(nc.semaphore(name))

    def take(eng, sem, n=1):
        eng.wait_ge(sem, n).then_inc(sem, -n)

    own = {e: semaphore("own_" + n) for e, n in ((pe, "pe"), (act, "act"), (dve, "dve"), (pool, "pool"))}
    pair = {(a, b): semaphore(f"{m}_to_{n}")
            for a, m in ((pe, "pe"), (act, "act"), (dve, "dve"), (pool, "pool"))
            for b, n in ((pe, "pe"), (act, "act"), (dve, "dve"), (pool, "pool"), (sp, "sp")) if a is not b}
    n_fetched = [0]

    def done(eng, ins):
        ins.then_inc(own[eng], 1)
        take(eng, own[eng])

    def tell(eng, ins, *sems):
        done(eng, ins)
        for s in sems:
            eng.sem_inc(s, 1)

    def hand(ins, src, dst):
        ins.then_inc(pair[src, dst], 1)
        take(dst, pair[src, dst])

    def fetched(eng, *dmas):
        landed = semaphore(f"landed{n_fetched[0]}")
        n_fetched[0] += 1
        for d in dmas:
            d.then_inc(landed, 16)
        take(eng, landed, 16 * len(dmas))

    def sbuf(st, name, shape, dt=f32):
        return st.enter_context(nc.sbuf_tensor(name, shape, dt))

    def psum(st, name, shape, dt=f32):
        return st.enter_context(nc.psum_tensor(name, shape, dt))

    def scratch(name, shape, dt):
        return nc.dram_tensor(name, shape, dt, kind="Internal").ap()

    k_rows = scratch("k_rows", (HEADS * HROWS, NKEY), bf16)
    q_rows = scratch("q_rows", (HEADS * KROWS, TOK), bf16)
    v_raw = scratch("v_raw", (NKEY // KT, KT, DIM), f32)
    v_int = scratch("v_int", (HEADS, NCH, KT, CT * HDIM), bf16)
    attn_rows = scratch("attn_rows", (TOK, DIM), f32)

    def token_tiles(x):
        return x.rearrange("(t p) d -> p t d", p=TT)

    def bcast(vec, n):
        return vec.rearrange("(a n) -> a n", a=1).to_broadcast([n, vec.shape[0]])

    ident = sbuf(ctx, "ident", [P, P])
    ident_b = sbuf(ctx, "ident_b", [P, P], bf16)
    resid = sbuf(ctx, "resid", [TT, NTT, DIM])
    v_scale = sbuf(ctx, "v_scale", [KT, DIM])
    summary = sbuf(ctx, "summary", [BATCH, DIM])
    v_inv = sbuf(ctx, "v_inv", [KT, DIM])

    done(pool, pool.memset(ident[:, :], 0.0))
    done(pool, pool.affine_select(out=ident[:, :], in_=ident[:, :], compare_op=ALU.not_equal, fill=1.0,
                                  base=0, pattern=[[-1, P]], channel_multiplier=1))
    pool.sem_inc(pair[pool, dve], 1)
    take(dve, pair[pool, dve])
    hand(dve.tensor_copy(ident_b[:, :], ident[:, :]), dve, pe)
    fetched(dve, sp.dma_start(resid[:, :, :], token_tiles(t["x"])))

    def layer_norm(st, x, h, tag):
        stats = sbuf(st, "ln_stats" + tag, [TT, NTT, 6])
        mv = sbuf(st, "ln_mv" + tag, [TT, NTT, 2])
        std = sbuf(st, "ln_std" + tag, [TT, NTT])
        for i in range(NTT):
            last = dve.bn_stats(stats[:, i, :], x[:, i, :])
        done(dve, last)
        for i in range(NTT):
            last = dve.bn_aggr(mv[:, i, :], stats[:, i, :])
        done(dve, last)
        hand(dve.tensor_scalar(std[:, :], mv[:, :, 1], EPS, None, ALU.add), dve, act)
        hand(act.activation(std[:, :], std[:, :], ACT.Sqrt), act, dve)
        done(dve, dve.reciprocal(std[:, :], std[:, :]))
        for i in range(NTT):
            last = dve.tensor_scalar(h[:, i, :], x[:, i, :], mv[:, i, 0:1], std[:, i:i + 1],
                                     ALU.subtract, ALU.mult)
        return last

    def transpose_tokens(h, hT, ps):
        for c in range(NC):
            for i in range(NTT):
                last = pe.transpose(ps[:, 2 * c + i // TPH, (i % TPH) * TT:(i % TPH + 1) * TT],
                                    h[:, i, c * P:(c + 1) * P], ident[0:TT, 0:TT])
        hand(last, pe, dve)
        for c in range(NC):
            last = dve.tensor_copy(hT[:, c, :].rearrange("p (b n) -> p b n", b=2), ps[:, 2 * c:2 * c + 2, 0:HALF])
        return last

    def project_tokens(hT, w, ps, width=DIM):
        for i in range(NTT):
            for c in range(NC):
                last = pe.matmul(ps[:, i, 0:width], hT[:, c, i * TT:(i + 1) * TT], w[:, c, 0:width],
                                 start=(c == 0), stop=(c == NC - 1))
        return last

    def quantise(x, amax, scale, groups):
        xg = x.rearrange("p (g d) -> p g d", d=HDIM)
        n = xg.shape[0]
        sb_ = scale.rearrange("p (g o) -> p g o", o=1).to_broadcast([n, groups, HDIM])
        done(dve, dve.tensor_reduce(amax, xg, axis=AX.X, op=ALU.max, apply_absolute_value=True))
        done(dve, dve.tensor_scalar(scale, amax, 1.0 / QMAX, TINY, ALU.mult, ALU.max))
        done(dve, dve.reciprocal(amax, scale))
        done(dve, dve.tensor_tensor(xg, xg, amax.rearrange("p (g o) -> p g o", o=1).to_broadcast([n, groups, HDIM]),
                                    ALU.mult))
        done(dve, dve.tensor_scalar(x, x, ROUND, ROUND, ALU.add, ALU.subtract))
        return xg, sb_

    with ExitStack() as st:
        h = sbuf(st, "h", [TT, NTT, DIM])
        hT = sbuf(st, "hT", [P, NC, TOK])
        wq = sbuf(st, "wq", [P, NC, DIM])
        bq = sbuf(st, "bq", [TT, DIM])
        q = sbuf(st, "q", [TT, NTT, DIM])
        rest = sbuf(st, "q_rest", [TT, NTT, DIM])
        amax = sbuf(st, "q_amax", [TT, NTT * HEADS])
        scale = sbuf(st, "q_scale", [TT, NTT * HEADS])
        parts = sbuf(st, "q_parts", [TT, NTT, HEADS, KROWS], bf16)
        rows = sbuf(st, "q_rows_sb", [KROWS, HEADS, TOK], bf16)
        ps = psum(st, "ps_q", [P, 4, BANK])
        psp = ps[0:TT, :, :].rearrange("p b (i n) -> p (b i) n", n=DIM)
        psr = [psum(st, f"ps_qrows{i}", [KROWS, 2 * BANK], bf16) for i in range(4)]
        fetched(pe, sp.dma_start(wq[:, :, :], t["L0_xattn_Wq"].rearrange("(c p) n -> p c n", p=P)))
        fetched(dve, sp.dma_start(bq[:, :], bcast(t["L0_xattn_bq"], TT)))
        hand(layer_norm(st, resid, h, "q"), dve, pe)
        hand(transpose_tokens(h, hT, ps), dve, pe)
        hand(project_tokens(hT, wq, psp), pe, dve)
        done(dve, dve.tensor_tensor(q[:, :, :], psp, bq[:, :].rearrange("p (o n) -> p o n", o=1)
                                    .to_broadcast([TT, NTT, DIM]), ALU.add))
        flat = q[:, :, :].rearrange("p t n -> p (t n)")
        done(dve, dve.tensor_scalar(flat, flat, 1.0 / math.sqrt(HDIM), None, ALU.mult))
        xg, sb_ = quantise(flat, amax[:, :], scale[:, :], NTT * HEADS)
        done(dve, dve.tensor_tensor(xg, xg, sb_, ALU.mult))
        qh = q[:, :, :].rearrange("p t (h d) -> p t h d", d=HDIM)
        rh = rest[:, :, :].rearrange("p t (h d) -> p t h d", d=HDIM)

        def part(i):
            return parts[:, :, :, i * HDIM:(i + 1) * HDIM]

        def per_tile(fn):
            for i in range(NTT):
                last = fn(i)
            done(dve, last)
        per_tile(lambda i: dve.tensor_copy(part(0)[:, i], qh[:, i]))
        per_tile(lambda i: dve.tensor_tensor(rh[:, i], qh[:, i], part(0)[:, i], ALU.subtract))
        per_tile(lambda i: dve.tensor_copy(part(3)[:, i], rh[:, i]))
        per_tile(lambda i: dve.tensor_tensor(part(5)[:, i], rh[:, i], part(3)[:, i], ALU.subtract))
        per_tile(lambda i: dve.tensor_copy(part(1)[:, i], part(0)[:, i]))
        per_tile(lambda i: dve.tensor_copy(part(2)[:, i], part(0)[:, i]))
        for i in range(NTT):
            last = dve.tensor_copy(part(4)[:, i], part(3)[:, i])
        hand(last, dve, pe)
        for hd in range(HEADS):
            dst = psr[hd % 4]
            if hd >= 4:
                take(pe, pair[dve, pe])
            for i in range(NTT):
                last = pe.transpose(dst[:, i * TT:(i + 1) * TT], parts[:, i, hd, :], ident_b[0:TT, 0:TT])
            hand(last, pe, dve)
            copied = dve.tensor_copy(rows[:, hd, :], dst[:, 0:TOK])
            if hd < HEADS - 1:
                copied.then_inc(pair[dve, pe], 1)
        take(pe, pair[dve, pe], 3)
        hand(copied, dve, sp)
        fetched(sp, sp.dma_start(q_rows.rearrange("(h r) n -> r h n", r=KROWS), rows[:, :, :]))
    nc.all_engine_barrier()

    ctxT = t["ctxT"].rearrange("(c p) n -> p c n", p=P)
    BLK = 2 * HROWS
    NBLK = HEADS * HROWS // BLK
    with ExitStack() as st:
        wkv = sbuf(st, "wkv", [P, NC, 2 * DIM])
        bkv = sbuf(st, "bkv", [KT, 2 * DIM])
        cx = [sbuf(st, f"cx{u}", [P, NC, GK]) for u in range(2)]
        kv = [sbuf(st, f"kv{u}", [KT, GEN, 2 * DIM]) for u in range(2)]
        kq = [sbuf(st, f"kq{u}", [KT, GEN, DIM]) for u in range(2)]
        rest = [sbuf(st, f"krest{u}", [KT, GEN, DIM]) for u in range(2)]
        kr = sbuf(st, "k_round", [KT, GEN * DIM])
        amax = sbuf(st, "k_amax", [KT, GEN * HEADS])
        scale = sbuf(st, "k_scale", [KT, GEN * HEADS])
        parts = [sbuf(st, f"kparts{u}", [KT, GEN, HEADS, HROWS], bf16) for u in range(2)]
        rows = [sbuf(st, f"krows{u}", [BLK, NBLK, GK], bf16) for u in range(2)]
        v_top = sbuf(st, "v_top", [KT, DIM])
        v_amax = sbuf(st, "v_amax", [KT, DIM])
        v_all = sbuf(st, "v_all", [KT, DIM])
        psk = psum(st, "ps_kv", [KT, GEN, BANK])
        pst = psum(st, "ps_krows", [BLK, NBLK, GEN, P], bf16)
        cx_ld = [semaphore(f"cx_ld{u}") for u in range(2)]
        cx_free = [semaphore(f"cx_free{u}") for u in range(2)]
        kv_ready, kv_bank_free = semaphore("kv_ready"), semaphore("kv_bank_free")
        v_ready, v_out = semaphore("v_ready"), [semaphore(f"v_out{u}") for u in range(2)]
        kq_ready, kq_free = semaphore("kq_ready"), semaphore("kq_free")
        high_ready, rest_ready = semaphore("high_ready"), semaphore("rest_ready")
        mid_ready, low_ready = semaphore("mid_ready"), semaphore("low_ready")
        rows_ready, rows_free = semaphore("rows_ready"), semaphore("rows_free")
        rows_out = [semaphore(f"rows_out{u}") for u in range(2)]

        fetched(pe, sp.dma_start(wkv[:, :, :], t["L0_xattn_Wkv"].rearrange("(c p) n -> p c n", p=P)))
        fetched(dve, sp.dma_start(bkv[:, :], bcast(t["L0_xattn_bkv"], KT)))
        done(dve, dve.memset(v_amax[:, :], 0.0))
        for u in range(2):
            sp.sem_inc(v_out[u], 16)
            act.sem_inc(rows_out[u], 16)
        dve.sem_inc(kv_bank_free, GEN)
        pool.sem_inc(kq_free, 2)
        act.sem_inc(rows_free, 1)

        def load_ctx(n, u):
            sp.dma_start(cx[u][:, :, :], ctxT[:, :, bass.ds(n * GK, GK)]).then_inc(cx_ld[u], 16)

        def project(u):
            take(pe, cx_ld[u], 16)
            for i in range(GEN):
                take(pe, kv_bank_free)
                for c in range(NC):
                    last = pe.matmul(psk[:, i, :], cx[u][:, c, i * KT:(i + 1) * KT], wkv[:, c, :],
                                     start=(c == 0), stop=(c == NC - 1))
                last.then_inc(kv_ready, 1)

        def split(n, u):
            take(dve, v_out[u], 16)
            for i in range(GEN):
                take(dve, kv_ready)
                last = dve.tensor_tensor(kv[u][:, i, :], psk[:, i, :], bkv[:, :], ALU.add)
                if i < GEN - 1:
                    last.then_inc(kv_bank_free, 1)
            tell(dve, last, kv_bank_free, cx_free[u], v_ready)
            take(sp, v_ready)
            sp.dma_start(v_raw[bass.ds(n * GEN, GEN), :, :].rearrange("t p d -> p t d"),
                         kv[u][:, :, DIM:]).then_inc(v_out[u], 16)
            kg = kv[u][:, :, 0:DIM].rearrange("p t (h d) -> p t h d", d=HDIM)
            sg = scale[:, :].rearrange("p (t h) -> p t h", t=GEN)
            done(dve, dve.tensor_reduce(amax[:, :].rearrange("p (t h) -> p t h", t=GEN), kg, axis=AX.X,
                                        op=ALU.max, apply_absolute_value=True))
            done(dve, dve.tensor_scalar(scale[:, :], amax[:, :], 1.0 / QMAX, TINY, ALU.mult, ALU.max))
            done(dve, dve.reciprocal(amax[:, :], scale[:, :]))
            s3 = scale[:, :].rearrange("p (g o) -> p g o", o=1).to_broadcast([KT, GEN * HEADS, HDIM])
            k3 = kr[:, :].rearrange("p (g d) -> p g d", d=HDIM)
            s4 = amax[:, :].rearrange("p (t h o) -> p t h o", t=GEN, o=1).to_broadcast([KT, GEN, HEADS, HDIM])
            k4 = kr[:, :].rearrange("p (t h d) -> p t h d", t=GEN, d=HDIM)
            done(dve, dve.tensor_tensor(k4, kg, s4, ALU.mult))
            done(dve, dve.tensor_scalar(kr[:, :], kr[:, :], ROUND, ROUND, ALU.add, ALU.subtract))
            take(dve, kq_free)
            q3 = kq[u][:, :, :].rearrange("p t (h d) -> p (t h) d", d=HDIM)
            dve.tensor_tensor(q3, k3, s3, ALU.mult).then_inc(kq_ready, 1)
            done(dve, dve.tensor_reduce(v_top[:, :], kv[u][:, :, DIM:].rearrange("p t d -> p d t"), axis=AX.X,
                                        op=ALU.max, apply_absolute_value=True))
            done(dve, dve.tensor_tensor(v_amax[:, :], v_amax[:, :], v_top[:, :], ALU.max))

            def part(i):
                return parts[u][:, :, :, i * HDIM:(i + 1) * HDIM].rearrange("p t h d -> p (t h) d")
            r3 = rest[u][:, :, :].rearrange("p t (h d) -> p (t h) d", d=HDIM)
            take(act, kq_ready)
            act.activation(part(0), q3, ACT.Copy).then_inc(high_ready, 1)
            take(pool, high_ready)
            tell(pool, pool.tensor_tensor(r3, q3, part(0), ALU.subtract), rest_ready, kq_free)
            return part, r3

        def split_low(u, part, r3):
            take(act, rest_ready)
            act.activation(part(1), r3, ACT.Copy).then_inc(mid_ready, 1)
            take(pool, mid_ready)
            pool.tensor_tensor(part(2), r3, part(1), ALU.subtract).then_inc(low_ready, 1)

        def transpose_rows(n, u):
            take(pe, low_ready)
            take(pe, rows_free)
            flat = parts[u][:, :, :, :].rearrange("p t h r -> p t (h r)")
            for i in range(GEN):
                for b in range(NBLK):
                    last = pe.transpose(pst[:, b, i, 0:KT], flat[:, i, b * BLK:(b + 1) * BLK], ident_b[0:KT, 0:KT])
            last.then_inc(rows_ready, 1)
            take(act, rows_ready)
            take(act, rows_out[u], 16)
            tell(act, act.activation(rows[u][:, :, :].rearrange("p b (t k) -> p (b t) k", k=KT),
                                     pst[:, :, :, :].rearrange("p b t k -> p (b t) k")[:, :, 0:KT], ACT.Copy),
                 rows_free)
            act.dma_start(k_rows.rearrange("(b p) n -> p b n", p=BLK)[:, :, bass.ds(n * GK, GK)],
                          rows[u][:, :, :]).then_inc(rows_out[u], 16)

        def step(n, u, load, more, before):
            if more:
                project(1 - u)
            part, r3 = split(n, u)
            take(sp, cx_free[u])
            if load:
                load_ctx(n + 2, u)
            if before:
                transpose_rows(n - 1, 1 - u)
            split_low(u, part, r3)

        load_ctx(0, 0)
        load_ctx(1, 1)
        project(0)
        step(0, 0, True, True, False)
        with nc.Fori(0, (NGEN - 4) // 2) as i:
            step(i * 2 + 1, 1, True, True, True)
            step(i * 2 + 2, 0, True, True, True)
        step(NGEN - 3, 1, True, True, True)
        step(NGEN - 2, 0, False, True, True)
        step(NGEN - 1, 1, False, False, True)
        transpose_rows(NGEN - 1, 1)
        for u in range(2):
            take(sp, v_out[u], 16)
            take(act, rows_out[u], 16)
        take(pool, kq_free, 2)
        take(pe, kv_bank_free, GEN)
        take(pe, rows_free)
        done(dve, dve.tensor_copy(v_top[:, :], v_amax[:, :]))
        hand(dve.tensor_copy(v_amax[:, :], v_top[:, :]), dve, pool)
        hand(pool.partition_all_reduce(v_all[:, :], v_amax[:, :], KT, bass.bass_isa.ReduceOp.absmax), pool, dve)
        done(dve, dve.tensor_scalar(v_scale[:, :], v_all[:, :], 1.0 / QMAX, TINY, ALU.mult, ALU.max))
        done(dve, dve.reciprocal(v_inv[:, :], v_scale[:, :]))
    nc.all_engine_barrier()

    with ExitStack() as st:
        vf = [sbuf(st, f"vf{u}", [KT, CT, DIM]) for u in range(2)]
        vq = [sbuf(st, f"vq{u}", [KT, HEADS, CT, HDIM], bf16) for u in range(2)]
        vf_ld = [semaphore(f"vf_ld{u}") for u in range(2)]
        vf_free = [semaphore(f"vf_free{u}") for u in range(2)]
        vq_ready = semaphore("vq_ready")
        vq_out = [semaphore(f"vq_out{u}") for u in range(2)]
        for u in range(2):
            dve.sem_inc(vq_out[u], 16)
            dve.sem_inc(vf_free[u], 1)

        def quantise_values(j, u):
            take(sp, vf_free[u])
            sp.dma_start(vf[u][:, :, :], v_raw[bass.ds(j * CT, CT), :, :].rearrange("t p d -> p t d"))\
              .then_inc(vf_ld[u], 16)
            take(dve, vf_ld[u], 16)
            done(dve, dve.tensor_tensor(vf[u][:, :, :], vf[u][:, :, :],
                                        v_inv[:, :].rearrange("p (o d) -> p o d", o=1)
                                        .to_broadcast([KT, CT, DIM]), ALU.mult))
            take(dve, vq_out[u], 16)
            tell(dve, dve.tensor_scalar(vq[u][:, :, :, :].rearrange("p h t d -> p t h d"),
                                        vf[u][:, :, :].rearrange("p t (h d) -> p t h d", d=HDIM),
                                        ROUND, ROUND, ALU.add, ALU.subtract), vf_free[u], vq_ready)
            take(act, vq_ready)
            act.dma_start(v_int.rearrange("h j p n -> p h j n")[:, :, bass.ds(j, 1), :],
                          vq[u][:, :, :, :].rearrange("p h t d -> p h (t d)")
                          .rearrange("p h (o n) -> p h o n", o=1)).then_inc(vq_out[u], 16)

        with nc.Fori(0, NCH // 2) as i:
            for u in range(2):
                quantise_values(i * 2 + u, u)
        for u in range(2):
            take(act, vq_out[u], 16)
            take(sp, vf_free[u])
    nc.all_engine_barrier()

    SLOTS = 4
    LAG = 2
    with ExitStack() as st:
        k1 = [sbuf(st, f"k1_{u}", [KROWS, CK], bf16) for u in range(2)]
        k2 = [sbuf(st, f"k2_{u}", [MROWS, CK], bf16) for u in range(2)]
        q1 = sbuf(st, "q1", [KROWS, TOK], bf16)
        q2 = sbuf(st, "q2", [MROWS, TOK], bf16)
        vt = [sbuf(st, f"vt{u}", [KT, CT, HDIM], bf16) for u in range(2)]
        e = [sbuf(st, f"e{i}", [KT, 2, HALF]) for i in range(SLOTS)]
        r = [sbuf(st, f"r{i}", [KT, 2, HALF], bf16) for i in range(SLOTS)]
        ones = sbuf(st, "ones", [KT, SUMROWS])
        zeros = sbuf(st, "zeros", [KT, HALF], bf16)
        unit_max = sbuf(st, "unit_max", [QB, NQB, NPIECE])
        chunk_max = sbuf(st, "chunk_max", [QB, NQB])
        run_max = sbuf(st, "run_max", [QB, NQB])
        shift = sbuf(st, "shift", [QB, NQB])
        shift_parts = sbuf(st, "shift_parts", [QB, NQB, PARTS], bf16)
        av = sbuf(st, "av", [P, HALF])
        inv_z = sbuf(st, "inv_z", [TT, TPH, 2])
        head_out = sbuf(st, "head_out", [TT, NTT, HDIM])
        decay = sbuf(st, "decay", [P, 1])
        keep = sbuf(st, "keep", [P, LCTX])
        ones_c = sbuf(st, "ones_c", [P, LCTX])
        weight = sbuf(st, "weight", [P, LCTX])
        wsum = sbuf(st, "wsum", [P, 1])
        cb = [sbuf(st, f"cb{u}", [P, NC, LCTX]) for u in range(2)]
        prod = sbuf(st, "prod", [P, LCTX])
        csum = sbuf(st, "csum", [P, NC])
        ctx_sum = sbuf(st, "ctx_sum", [P, NC, BATCH])
        cb_ld, cb_free = ([semaphore(f"{n}{u}") for u in range(2)] for n in ("cb_ld", "cb_free"))

        ps1 = [psum(st, f"ps_sweep1_{i}", [P, 2, BANK]) for i in range(2)]
        ps2 = [psum(st, f"ps_sweep2_{i}", [KT, BANK]) for i in range(3)]
        psav = psum(st, "ps_av", [P, BANK])
        k1_ld, k1_free, k2_ld, k2_free, v_ld, v_free = (
            [semaphore(f"{n}{u}") for u in range(2)]
            for n in ("k1_ld", "k1_free", "k2_ld", "k2_free", "v_ld", "v_free"))
        s2_ready, s2_free, e_ready, e_free, r_ready, s1_ready, s1_free, q1_free, q1_ld, q2_ld, head_stored = (
            semaphore(n) for n in ("s2_ready", "s2_free", "e_ready", "e_free", "r_ready", "s1_ready", "s1_free",
                                   "q1_free", "q1_ld", "q2_ld", "head_stored"))

        done(pool, pool.memset(zeros[:, :], 0.0))
        for u in range(2):
            done(pool, pool.memset(k2[u][KROWS:MROWS, :], 1.0))
        hand(pool.memset(ones[:, :], 1.0), pool, pe)
        done(dve, dve.memset(run_max[:, :], -3.0e38))
        for u in range(2):
            dve.sem_inc(k1_free[u], 1)
            dve.sem_inc(k2_free[u], 1)
            dve.sem_inc(v_free[u], 1)
            dve.sem_inc(cb_free[u], 1)
        dve.sem_inc(s2_free, 3)
        dve.sem_inc(s1_free, 2)
        dve.sem_inc(e_free, SLOTS)
        dve.sem_inc(head_stored, 16)

        done(dve, dve.memset(ones_c[:, :], 1.0))
        fetched(act, sp.dma_start(decay[:, :], bcast(t["L1_xattn_decay"], P)))
        hand(act.activation(decay[:, :], decay[:, :], ACT.Sigmoid), act, dve)
        done(dve, dve.tensor_scalar(keep[:, :], ones_c[:, :], decay[:, 0:1], None, ALU.mult))
        done(dve, dve.tensor_tensor_scan(weight[:, :], keep[:, :], ones_c[:, :], 0.0, ALU.mult, ALU.add))
        done(dve, dve.tensor_reduce(wsum[:, :], weight[:, :], axis=AX.X, op=ALU.add))
        done(dve, dve.tensor_copy(keep[:, :], weight[:, ::-1]))

        def weigh_context(b, u):
            take(sp, cb_free[u])
            sp.dma_start(cb[u][:, :, :], ctxT[:, :, bass.ds(b * LCTX, LCTX)]).then_inc(cb_ld[u], 16)
            take(dve, cb_ld[u], 16)
            for c in range(NC):
                done(dve, dve.tensor_tensor_reduce(out=prod[:, :], in0=cb[u][:, c, :], in1=keep[:, :], scale=1.0,
                                                   scalar=0.0, op0=ALU.mult, op1=ALU.add,
                                                   accum_out=csum[:, c:c + 1]))
            dve.sem_inc(cb_free[u], 1)
            done(dve, dve.tensor_copy(ctx_sum[:, :, bass.ds(b, 1)], csum[:, :].rearrange("p (c o) -> p c o", o=1)))

        def load_keys(dst, sem, head, j):
            at = head * HROWS
            for lo, n in ((0, HROWS), (HROWS, 2 * HDIM), (HROWS + 2 * HDIM, HDIM)):
                sp.dma_start(dst[lo:lo + n, :], k_rows[bass.ds(at, n), bass.ds(j * CK, CK)]).then_inc(sem, 16)

        def load_queries(dst, head, sem):
            act.dma_start(dst[0:KROWS, :], q_rows[bass.ds(head * KROWS, KROWS), :]).then_inc(sem, 16)

        def chunk(h1, h2, j, u):
            if h1 is not None:
                take(sp, k1_free[u])
                load_keys(k1[u], k1_ld[u], h1, j)
            if h2 is not None:
                take(sp, k2_free[u])
                load_keys(k2[u], k2_ld[u], h2, j)
                take(sp, v_free[u])
                sp.dma_start(vt[u][:, :, :].rearrange("p t d -> p (t d)"),
                             v_int[bass.ds(h2, 1), bass.ds(j, 1), :, :].rearrange("h j p n -> (h j p) n"))\
                  .then_inc(v_ld[u], 16)
                take(pe, k2_ld[u], 48)

            def scores(i):
                for g in range(2):
                    ps = ps2[(2 * i + g) % 3]
                    take(pe, s2_free)
                    pe.matmul(ps[:, 0:HALF], k2[u][:, i * KT:(i + 1) * KT], q2[:, g * HALF:(g + 1) * HALF],
                              start=True, stop=True).then_inc(s2_ready, 1)
                    if g == 0:
                        take(act, e_free)
                    take(act, s2_ready)
                    exp = act.activation(e[i % SLOTS][:, g, :], ps[:, 0:HALF], ACT.Exp)
                    if g == 0:
                        exp.then_inc(s2_free, 1)
                    else:
                        tell(act, exp, s2_free, e_ready)

            def rounded(i):
                take(dve, e_ready)
                if i == CT - 1:
                    dve.sem_inc(k2_free[u], 1)
                dve.tensor_scalar(r[i % SLOTS][:, :, :], e[i % SLOTS][:, :, :], ROUND, ROUND,
                                  ALU.add, ALU.subtract).then_inc(r_ready, 1)

            def unit(n):
                piece, b = divmod(n, NQB)
                if n == 0:
                    take(pe, k1_ld[u], 48)
                take(pe, s1_free)
                for i in range(2):
                    at = (piece * 2 + i) * SB
                    last = pe.matmul(ps1[(n + u) % 2][:, i, 0:SB], q1[:, b * QB:(b + 1) * QB], k1[u][:, at:at + SB],
                                     start=True, stop=True)
                last.then_inc(s1_ready, 1)
                take(dve, s1_ready)
                top = dve.tensor_reduce(unit_max[:, b, piece:piece + 1], ps1[(n + u) % 2][:, :, 0:SB], axis=AX.XY, op=ALU.max)
                if n < NQB * NPIECE - 1:
                    top.then_inc(s1_free, 1)
                    return
                tell(dve, top, s1_free, k1_free[u])
                done(dve, dve.tensor_reduce(chunk_max[:, :], unit_max[:, :, :], axis=AX.X, op=ALU.max))
                done(dve, dve.tensor_tensor(run_max[:, :], run_max[:, :], chunk_max[:, :], ALU.max))

            def sums(i):
                s = i % SLOTS
                if i == 0:
                    take(pe, v_ld[u], 16)
                take(pe, r_ready)
                for g in range(2):
                    c = g * SUMROWS
                    last = pe.matmul(psav[c:c + HDIM, 0:HALF], vt[u][:, i, :], r[s][:, g, :],
                                     start=False, stop=False, skip_group_check=True, tile_position=(0, c))
                if i == CT - 1:
                    last.then_inc(v_free[u], 1)
                for g in range(2):
                    c = (2 + g) * SUMROWS
                    last = pe.matmul(psav[c:c + SUMROWS, 0:HALF], ones[:, :], e[s][:, g, :],
                                     start=False, stop=False, skip_group_check=True, tile_position=(0, c))
                last.then_inc(e_free, 1)

            n = 0
            for i in range(CT):
                if h2 is not None:
                    scores(i)
                    rounded(i)
                if h1 is not None and i % 8 != 7:
                    unit(n)
                    n += 1
                if h2 is not None and i >= LAG:
                    sums(i - LAG)
            if h2 is not None:
                for i in range(CT - LAG, CT):
                    sums(i)

        def start_second_sweep(head):
            load_queries(q2, head, q2_ld)
            done(dve, dve.tensor_scalar(shift[:, :], run_max[:, :], -1.0, LOG255, ALU.mult, ALU.add))
            done(dve, dve.tensor_copy(shift_parts[:, :, 0], shift[:, :]))
            done(dve, dve.tensor_tensor(shift[:, :], shift[:, :], shift_parts[:, :, 0], ALU.subtract))
            done(dve, dve.tensor_copy(shift_parts[:, :, 1], shift[:, :]))
            hand(dve.tensor_tensor(shift_parts[:, :, 2], shift[:, :], shift_parts[:, :, 1], ALU.subtract), dve, pe)
            take(pe, s1_free, 2)
            for b in range(NQB):
                last = pe.matmul(ps1[0][KROWS:MROWS, b // 4, (b % 4) * QB:(b % 4 + 1) * QB], shift_parts[:, b, :],
                                 ident_b[:, :], start=True, stop=True, tile_position=(0, KROWS))
            hand(last, pe, dve)
            dve.tensor_copy(q2[KROWS:MROWS, 0:BANK], ps1[0][KROWS:MROWS, 0, :])
            tell(dve, dve.tensor_copy(q2[KROWS:MROWS, BANK:TOK], ps1[0][KROWS:MROWS, 1, 0:TOK - BANK]),
                 pair[dve, pe], s1_free, q1_free)
            take(pe, pair[dve, pe])
            take(pe, q2_ld, 16)
            done(dve, dve.memset(run_max[:, :], -3.0e38))

        def copy_sums():
            take(act, e_free, SLOTS)
            act.sem_inc(e_free, SLOTS)
            hand(act.activation(av[:, :], psav[:, 0:HALF], ACT.Copy), act, pe)

        def clear_sums():
            for g in range(4):
                pe.matmul(psav[g * SUMROWS:(g + 1) * SUMROWS, 0:HALF], zeros[:, 0:SUMROWS], zeros[:, :],
                          start=True, stop=True, tile_position=(0, g * SUMROWS))

        def finish_head(head):
            for i in range(TPH):
                last = pe.transpose(ps1[1][0:TT, 0, i * P:(i + 1) * P], av[:, i * TT:(i + 1) * TT], ident[:, :])
            hand(last, pe, dve)
            tr = ps1[1][0:TT, 0, :].rearrange("p (i g c) -> p i g c", i=TPH, c=SUMROWS)
            done(dve, dve.reciprocal(inv_z[:, :, :], tr[:, :, 2:4, 0]))
            take(dve, head_stored, 16)
            for g in range(2):
                last = dve.tensor_tensor(head_out[:, g * TPH:(g + 1) * TPH, :], tr[:, :, g, 0:HDIM],
                                         inv_z[:, :, g:g + 1].to_broadcast([TT, TPH, HDIM]), ALU.mult)
            tell(dve, last, pair[dve, act], s1_free)
            take(act, pair[dve, act])
            act.dma_start(token_tiles(attn_rows)[:, :, bass.ds(head * HDIM, HDIM)],
                          head_out[:, :, :]).then_inc(head_stored, 16)

        def sweep(h1, h2, beside=None):
            with nc.Fori(0, NCH // 2) as jj:
                for u in range(2):
                    chunk(h1, h2, jj * 2 + u, u)
                    if beside is not None:
                        beside(jj * 2 + u)

        load_queries(q1, 0, q1_ld)
        take(pe, q1_ld, 16)
        sweep(0, None)
        start_second_sweep(0)
        pe.sem_inc(s1_free, 1)
        clear_sums()
        with nc.Fori(0, HEADS - 1) as hd:
            take(act, q1_free)
            load_queries(q1, hd + 1, q1_ld)
            take(pe, q1_ld, 16)
            sweep(hd + 1, hd)
            copy_sums()
            start_second_sweep(hd + 1)
            finish_head(hd)
            clear_sums()

        def weigh_two(j):
            weigh_context(j * 2, 0)
            weigh_context(j * 2 + 1, 1)

        sweep(None, HEADS - 1, weigh_two)
        copy_sums()
        take(pe, s1_free, 2)
        finish_head(HEADS - 1)
        take(act, head_stored, 16)
        take(act, q1_free)
        for u in range(2):
            take(sp, k1_free[u])
            take(sp, k2_free[u])
            take(sp, v_free[u])
            take(sp, cb_free[u])
        take(pe, s2_free, 3)
        take(pe, s1_free)
        take(act, e_free, SLOTS)
        nc.all_engine_barrier()

        w_in = sbuf(st, "w_in", [P, NC, DIM])
        w_out = sbuf(st, "w_out", [P, NC, DIM])
        b_in = sbuf(st, "b_in", [P, NC])
        b_out = sbuf(st, "b_out", [BATCH, DIM])
        mean = sbuf(st, "mean_state", [P, NC, BATCH])
        with nc.allow_non_contiguous_dma(reason="a bias as columns, once"):
            fetched(dve, sp.dma_start(b_in[:, :], t["L1_xattn_b_in"].rearrange("(c p) -> p c", p=P)),
                    sp.dma_start(b_out[:, :], bcast(t["L1_xattn_b_out"], BATCH)))
        fetched(pe, sp.dma_start(w_in[:, :, :], t["W_inT"].rearrange("(c p) n -> p c n", p=P)),
                sp.dma_start(w_out[:, :, :], t["W_outT"].rearrange("(c p) n -> p c n", p=P)))
        hand(dve.tensor_scalar(b_in[:, :], b_in[:, :], wsum[:, 0:1], None, ALU.mult), dve, pe)
        for m in range(NC):
            for c in range(NC):
                last = pe.matmul(ps1[0][:, m, 0:BATCH], w_in[:, c, m * P:(m + 1) * P], ctx_sum[:, c, :],
                                 start=(c == 0), stop=(c == NC - 1))
        hand(last, pe, dve)
        for m in range(NC):
            last = dve.tensor_scalar(mean[:, m, :], ps1[0][:, m, 0:BATCH], b_in[:, m:m + 1], 1.0 / LCTX,
                                     ALU.add, ALU.mult)
        hand(last, dve, pe)
        for c in range(NC):
            last = pe.matmul(ps1[1][0:BATCH, 0, 0:DIM], mean[:, c, :], w_out[:, c, :],
                             start=(c == 0), stop=(c == NC - 1))
        hand(last, pe, dve)
        done(dve, dve.tensor_tensor(summary[:, :], ps1[1][0:BATCH, 0, 0:DIM], b_out[:, :], ALU.add))
    nc.all_engine_barrier()

    def experts(st, tag, hT, comb, acc, n_exp, f, w_gu, w_dn):
        gu_w = [sbuf(st, f"gu_w{tag}{u}", [P, NC, 2 * f]) for u in range(2)]
        dn_w = [sbuf(st, f"dn_w{tag}{u}", [f, DIM]) for u in range(2)]
        gate = sbuf(st, "gate" + tag, [f, 2, HALF])
        hid = [sbuf(st, f"hid{tag}{u}", [f, 2, HALF]) for u in range(2)]
        cw = sbuf(st, "cw" + tag, [TT, NTT, 1])
        psg = psum(st, "ps_gate" + tag, [f, 2, BANK])
        psu = psum(st, "ps_up" + tag, [f, 2, BANK])
        psd = psum(st, "ps_down" + tag, [TT, NTT, DIM])
        gu_ld, dn_ld, dn_free = ([semaphore(f"{n}{tag}{u}") for u in range(2)] for n in ("gu_ld", "dn_ld", "dn_free"))
        gu_ready, up_free, gate_ready, hid_ready, dn_ready, dn_read = (
            semaphore(n + tag) for n in ("gu_ready", "up_free", "gate_ready", "hid_ready", "dn_ready", "dn_read"))
        dve.sem_inc(up_free, 1)
        dve.sem_inc(dn_read, 1)

        def load(x, u):
            sp.dma_start(gu_w[u][:, :, :].rearrange("p c n -> p (c n)"),
                         w_gu[bass.ds(x, 1), :, :].rearrange("e p n -> (e p) n")).then_inc(gu_ld[u], 16)
            sp.dma_start(dn_w[u][:, :], w_dn[bass.ds(x, 1), :, :].rearrange("e p n -> (e p) n"))\
              .then_inc(dn_ld[u], 16)

        def hidden(u):
            take(pe, gu_ld[u], 16)
            take(pe, up_free)
            for ps, lo in ((psg, 0), (psu, f)):
                for g in range(2):
                    for c in range(NC):
                        last = pe.matmul(ps[:, g, 0:HALF], gu_w[u][:, c, lo:lo + f],
                                         hT[:, c, g * HALF:(g + 1) * HALF], start=(c == 0), stop=(c == NC - 1))
            last.then_inc(gu_ready, 1)
            take(act, gu_ready)
            act.activation(gate[:, :, :], psg[:, :, 0:HALF], ACT.Silu).then_inc(gate_ready, 1)
            take(dve, gate_ready)
            tell(dve, dve.tensor_tensor(hid[u][:, :, :], psu[:, :, 0:HALF], gate[:, :, :], ALU.mult),
                 hid_ready, up_free)

        def step(x, u, ahead, more):
            if more:
                hidden(1 - u)
            take(pe, dn_ld[u], 16)
            take(pe, hid_ready)
            take(pe, dn_read)
            for i in range(NTT):
                last = pe.matmul(psd[:, i, :], hid[u][:, i // TPH, (i % TPH) * TT:(i % TPH + 1) * TT], dn_w[u][:, :],
                                 start=True, stop=True)
            last.then_inc(dn_ready, 1)
            done(dve, dve.tensor_copy(cw[:, :, :], comb[:, :, bass.ds(x, 1)]))
            take(dve, dn_ready)
            for i in range(NTT):
                last = dve.scalar_tensor_tensor(acc[:, i, :], psd[:, i, :], cw[:, i, :], acc[:, i, :],
                                                ALU.mult, ALU.add)
            tell(dve, last, dn_read, dn_free[u])
            take(sp, dn_free[u])
            if ahead:
                load(x + 2, u)

        load(0, 0)
        load(1, 1)
        hidden(0)
        with nc.Fori(0, (n_exp - 2) // 2) as i:
            step(i * 2, 0, True, True)
            step(i * 2 + 1, 1, True, True)
        step(n_exp - 2, 0, False, True)
        step(n_exp - 1, 1, False, False)
        take(pe, up_free)
        take(pe, dn_read)

    def top_mask(st, tag, vals, mask, n, k, pad):
        top = sbuf(st, "top" + tag, [TT, NTT, 8])
        marked = sbuf(st, "marked" + tag, [TT, NTT, n + pad])
        for i in range(NTT):
            last = dve.max(top[:, i, :], vals[:, i, :])
        done(dve, last)
        for i in range(NTT):
            last = dve.match_replace(out=marked[:, i, :], in_to_replace=top[:, i, :], in_values=vals[:, i, :],
                                     imm_value=-3.0e38)
        done(dve, last)
        done(dve, dve.tensor_tensor(mask[:, :, :], marked[:, :, pad:], vals[:, :, pad:], ALU.not_equal))
        return top

    PAD0, PAD1 = 8 - N_SEL0, 8 - N_SEL1
    with ExitStack() as st:
        h = sbuf(st, "h0", [TT, NTT, DIM])
        hT = sbuf(st, "hT0", [P, NC, TOK])
        comb = sbuf(st, "comb0", [TT, NTT, N_ALL0])
        with ExitStack() as s2:
            wp = sbuf(s2, "wp", [P, NC, DIM])
            gw = sbuf(s2, "gate_w", [P, NC, N_EXP0])
            bp = sbuf(s2, "bp", [TT, DIM])
            score = sbuf(s2, "score", [TT, NTT, N_EXP0 + PAD0])
            mask = sbuf(s2, "mask0", [TT, NTT, N_EXP0])
            total = sbuf(s2, "total0", [TT, NTT])
            ps = psum(s2, "ps_a", [P, 4, BANK])
            psb = psum(s2, "ps_b", [P, 4, BANK])
            psp = psb[0:TT, :, :].rearrange("p b (i n) -> p (b i) n", n=DIM)
            fetched(pe, sp.dma_start(wp[:, :, :], t["L0_xattn_Wp"].rearrange("(c p) n -> p c n", p=P)),
                    sp.dma_start(gw[:, :, :], t["L0_ffn_gate_w"].rearrange("(c p) n -> p c n", p=P)))
            fetched(dve, sp.dma_start(bp[:, :], bcast(t["L0_xattn_bp"], TT)),
                    sp.dma_start(h[:, :, :], token_tiles(attn_rows)))
            hand(dve.tensor_tensor(h[:, :, :], h[:, :, :], v_scale[0:TT, :].rearrange("p (o d) -> p o d", o=1)
                                   .to_broadcast([TT, NTT, DIM]), ALU.mult), dve, pe)
            hand(transpose_tokens(h, hT, ps), dve, pe)
            hand(project_tokens(hT, wp, psp), pe, dve)
            done(dve, dve.tensor_tensor(resid[:, :, :], resid[:, :, :], psp, ALU.add))
            done(dve, dve.tensor_tensor(resid[:, :, :], resid[:, :, :], bp[:, :].rearrange("p (o d) -> p o d", o=1)
                                        .to_broadcast([TT, NTT, DIM]), ALU.add))
            hand(layer_norm(s2, resid, h, "0"), dve, pe)
            hand(transpose_tokens(h, hT, ps), dve, pe)
            hand(project_tokens(hT, gw, psp, N_EXP0), pe, act)
            hand(dve.memset(score[:, :, 0:PAD0], 3.0), dve, act)
            hand(act.activation(score[:, :, PAD0:], psp[:, :, 0:N_EXP0], ACT.Sigmoid), act, dve)
            top_mask(s2, "0", score, mask, N_EXP0, N_SEL0, PAD0)
            done(dve, dve.tensor_tensor(mask[:, :, :], mask[:, :, :], score[:, :, PAD0:], ALU.mult))
            done(dve, dve.tensor_reduce(total[:, :], mask[:, :, :], axis=AX.X, op=ALU.add))
            done(dve, dve.tensor_scalar(total[:, :], total[:, :], 1e-20, None, ALU.add))
            done(dve, dve.reciprocal(total[:, :], total[:, :]))
            done(dve, dve.tensor_tensor(comb[:, :, 0:N_EXP0], mask[:, :, :],
                                        total[:, :].rearrange("p (t o) -> p t o", o=1)
                                        .to_broadcast([TT, NTT, N_EXP0]), ALU.mult))
            done(dve, dve.memset(comb[:, :, N_EXP0:], 1.0))
        nc.all_engine_barrier()
        experts(st, "0", hT, comb, resid, N_ALL0, F0, t["gu0"], t["dn0"])
    nc.all_engine_barrier()

    with ExitStack() as st:
        h = sbuf(st, "h1", [TT, NTT, DIM])
        hT = sbuf(st, "hT1", [P, NC, TOK])
        comb = sbuf(st, "comb1", [TT, NTT, N_ALL1])
        with ExitStack() as s2:
            sel = sbuf(s2, "sel", [BATCH, TOK])
            z = sbuf(s2, "z", [TT, NTT, DIM])
            gamma = sbuf(s2, "gamma", [TT, DIM])
            beta = sbuf(s2, "beta", [TT, DIM])
            rw = sbuf(s2, "router_w", [P, NC, N_EXP1])
            logit = sbuf(s2, "logit", [TT, NTT, N_EXP1 + PAD1])
            diff = sbuf(s2, "diff", [TT, NTT, N_EXP1])
            mask = sbuf(s2, "mask1", [TT, NTT, N_EXP1])
            total = sbuf(s2, "total1", [TT, NTT])
            ps = psum(s2, "ps_c", [P, 4, BANK])
            psb = psum(s2, "ps_d", [P, 4, BANK])
            psp = psb[0:TT, :, :].rearrange("p b (i n) -> p (b i) n", n=DIM)

            def over_tokens(v):
                return v[:, :].rearrange("p (o d) -> p o d", o=1).to_broadcast([TT, NTT, DIM])
            fetched(pe, sp.dma_start(rw[:, :, :], t["router_wT"].rearrange("(c p) n -> p c n", p=P)))
            fetched(dve, sp.dma_start(gamma[:, :], bcast(t["L1_xattn_gamma"], TT)),
                    sp.dma_start(beta[:, :], bcast(t["L1_xattn_beta"], TT)))
            done(pool, pool.memset(sel[:, :], 1.0))
            done(pool, pool.affine_select(out=sel[:, :], in_=sel[:, :], compare_op=ALU.is_ge, fill=0.0,
                                          base=0, pattern=[[1, TOK]], channel_multiplier=-SEQ))
            hand(pool.affine_select(out=sel[:, :], in_=sel[:, :], compare_op=ALU.is_ge, fill=0.0,
                                    base=SEQ - 1, pattern=[[-1, TOK]], channel_multiplier=SEQ), pool, pe)
            done(dve, layer_norm(s2, resid, z, "z"))
            for i in range(NTT):
                last = pe.matmul(psp[:, i, :], sel[:, i * TT:(i + 1) * TT], summary[:, :], start=True, stop=True)
            hand(last, pe, dve)
            done(dve, dve.tensor_tensor(z[:, :, :], z[:, :, :], psp, ALU.add))
            done(dve, layer_norm(s2, z, h, "y"))
            done(dve, dve.tensor_tensor(h[:, :, :], h[:, :, :], over_tokens(gamma), ALU.mult))
            done(dve, dve.tensor_tensor(h[:, :, :], h[:, :, :], over_tokens(beta), ALU.add))
            done(dve, dve.tensor_tensor(resid[:, :, :], resid[:, :, :], h[:, :, :], ALU.add))
            hand(layer_norm(s2, resid, h, "1"), dve, pe)
            hand(transpose_tokens(h, hT, ps), dve, pe)
            hand(project_tokens(hT, rw, psp, N_EXP1), pe, dve)
            done(dve, dve.memset(logit[:, :, 0:PAD1], 3.0e38))
            done(dve, dve.tensor_copy(logit[:, :, PAD1:], psp[:, :, 0:N_EXP1]))
            top = top_mask(s2, "1", logit, mask, N_EXP1, N_SEL1, PAD1)
            hand(dve.tensor_tensor(diff[:, :, :], logit[:, :, PAD1:],
                                   top[:, :, PAD1:PAD1 + 1].to_broadcast([TT, NTT, N_EXP1]), ALU.subtract), dve, act)
            hand(act.activation(diff[:, :, :], diff[:, :, :], ACT.Exp), act, dve)
            done(dve, dve.tensor_tensor(diff[:, :, :], diff[:, :, :], mask[:, :, :], ALU.mult))
            done(dve, dve.tensor_reduce(total[:, :], diff[:, :, :], axis=AX.X, op=ALU.add))
            done(dve, dve.reciprocal(total[:, :], total[:, :]))
            for half in range(2):
                done(dve, dve.tensor_tensor(comb[:, :, half::2], diff[:, :, :],
                                            total[:, :].rearrange("p (t o) -> p t o", o=1)
                                            .to_broadcast([TT, NTT, N_EXP1]), ALU.mult))
        nc.all_engine_barrier()
        experts(st, "1", hT, comb, resid, N_ALL1, F1, t["gu1"], t["dn1"])
    nc.all_engine_barrier()
    fetched(sp, sp.dma_start(token_tiles(t["out"]), resid[:, :, :]))
    ctx.close()


def kernel(**inputs):
    import numpy as np
    import concourse.bacc as bacc
    from concourse.bass_utils import run_bass_kernel_spmd as run

    a = {k: np.asarray(v) for k, v in inputs.items()}

    def gate_up(g, u):
        both = np.concatenate([g, u], axis=2)
        n, _, w = both.shape
        return both.reshape(n, NC, P, w).transpose(0, 2, 1, 3).reshape(n, P, NC * w)

    sg = a["L0_ffn_sg"].reshape(DIM, 2, F0).transpose(1, 0, 2)
    su = a["L0_ffn_su"].reshape(DIM, 2, F0).transpose(1, 0, 2)
    sd = a["L0_ffn_sd"].reshape(2, F0, DIM)
    w1 = a["L1_ffn_w1"].transpose(0, 2, 1).reshape(N_EXP1, DIM, 2, 2, F1)
    w1 = w1.transpose(2, 0, 3, 1, 4).reshape(2, N_ALL1, DIM, F1)
    w2 = a["L1_ffn_w2"].transpose(0, 2, 1).reshape(N_ALL1, F1, DIM)
    arrays = {
        "x": a["x"].reshape(TOK, DIM),
        "ctxT": a["ctx_2048"].reshape(NKEY, DIM).T,
        "gu0": gate_up(np.concatenate([a["L0_ffn_wg"], sg]), np.concatenate([a["L0_ffn_wu"], su])),
        "dn0": np.concatenate([a["L0_ffn_wd"], sd]),
        "gu1": gate_up(w1[0], w1[1]),
        "dn1": w2,
        "W_inT": a["L1_xattn_W_in"].T,
        "W_outT": a["L1_xattn_W_out"].T,
        "router_wT": a["L1_ffn_router_w"].T,
        "L1_xattn_decay": a["L1_xattn_decay"].reshape(1),
    }
    for n in ("L0_xattn_Wq", "L0_xattn_bq", "L0_xattn_Wkv", "L0_xattn_bkv", "L0_xattn_Wp", "L0_xattn_bp",
              "L0_ffn_gate_w", "L1_xattn_b_in", "L1_xattn_b_out", "L1_xattn_gamma", "L1_xattn_beta"):
        arrays[n] = a[n]
    arrays = {n: np.ascontiguousarray(v) for n, v in arrays.items()}

    nc = bacc.Bacc("TRN2", target_bir_lowering=False, num_devices=1)
    f32 = mybir.dt.float32
    t = {n: nc.dram_tensor("in_" + n, v.shape, f32, kind="ExternalInput").ap() for n, v in arrays.items()}
    t["out"] = nc.dram_tensor("out_0", (TOK, DIM), f32, kind="ExternalOutput").ap()
    build(nc, t)
    res = run(nc, [{"in_" + n: v for n, v in arrays.items()}], core_ids=[0])
    return np.asarray(res.results[0]["out_0"]).reshape(BATCH, SEQ, DIM)
```

```python
import math
from contextlib import ExitStack

import concourse.bass as bass
from concourse import mybir

BATCH, SEQ, DIM = 16, 56, 256
TOK = BATCH * SEQ
LCTX = 1500
NKEY = BATCH * LCTX
HEADS, HDIM = 16, 16
P = 128
NC = DIM // P
TT = 2 * SEQ
NTT = TOK // TT
HALF = TOK // 2
TPH = HALF // TT
KT = 125
GEN = 4
NGEN = NKEY // (KT * GEN)
GK = KT * GEN
CT = 24
CK = CT * KT
NCH = NKEY // CK
QB = P
NQB = TOK // QB
SB = 500
NPIECE = CK // (2 * SB)
PARTS = 3
HROWS = PARTS * HDIM
KROWS = 2 * HROWS
MROWS = KROWS + PARTS
SUMROWS = 32
N_EXP0, N_SEL0, F0 = 32, 6, 96
N_ALL0 = N_EXP0 + 2
N_EXP1, N_SEL1, F1 = 8, 2, 88
N_ALL1 = 2 * N_EXP1
BANK = 512
ROUND = 12582912.0
QMAX = 127.0
EPS = 1e-5
LOG255 = math.log(255.0)
TINY = 1e-8


def build(nc, t):
    f32, bf16 = mybir.dt.float32, mybir.dt.bfloat16
    ALU, ACT, AX = mybir.AluOpType, mybir.ActivationFunctionType, mybir.AxisListType
    pe, act, dve, pool, sp = nc.tensor, nc.scalar, nc.vector, nc.gpsimd, nc.sync
    ctx = ExitStack()

    def semaphore(name):
        return ctx.enter_context(nc.semaphore(name))

    def take(eng, sem, n=1):
        eng.wait_ge(sem, n).then_inc(sem, -n)

    own = {e: semaphore("own_" + n) for e, n in ((pe, "pe"), (act, "act"), (dve, "dve"), (pool, "pool"))}
    pair = {(a, b): semaphore(f"{m}_to_{n}")
            for a, m in ((pe, "pe"), (act, "act"), (dve, "dve"), (pool, "pool"))
            for b, n in ((pe, "pe"), (act, "act"), (dve, "dve"), (pool, "pool"), (sp, "sp")) if a is not b}
    n_fetched = [0]

    def done(eng, ins):
        ins.then_inc(own[eng], 1)
        take(eng, own[eng])

    def tell(eng, ins, *sems):
        done(eng, ins)
        for s in sems:
            eng.sem_inc(s, 1)

    def hand(ins, src, dst):
        ins.then_inc(pair[src, dst], 1)
        take(dst, pair[src, dst])

    def fetched(eng, *dmas):
        landed = semaphore(f"landed{n_fetched[0]}")
        n_fetched[0] += 1
        for d in dmas:
            d.then_inc(landed, 16)
        take(eng, landed, 16 * len(dmas))

    def sbuf(st, name, shape, dt=f32):
        return st.enter_context(nc.sbuf_tensor(name, shape, dt))

    def psum(st, name, shape, dt=f32):
        return st.enter_context(nc.psum_tensor(name, shape, dt))

    def scratch(name, shape, dt):
        return nc.dram_tensor(name, shape, dt, kind="Internal").ap()

    k_rows = scratch("k_rows", (HEADS * HROWS, NKEY), bf16)
    q_rows = scratch("q_rows", (HEADS * KROWS, TOK), bf16)
    v_raw = scratch("v_raw", (NKEY // KT, KT, DIM), f32)
    v_int = scratch("v_int", (HEADS, NCH, KT, CT * HDIM), bf16)
    attn_rows = scratch("attn_rows", (TOK, DIM), f32)

    def token_tiles(x):
        return x.rearrange("(t p) d -> p t d", p=TT)

    def bcast(vec, n):
        return vec.rearrange("(a n) -> a n", a=1).to_broadcast([n, vec.shape[0]])

    ident = sbuf(ctx, "ident", [P, P])
    ident_b = sbuf(ctx, "ident_b", [P, P], bf16)
    resid = sbuf(ctx, "resid", [TT, NTT, DIM])
    v_scale = sbuf(ctx, "v_scale", [KT, DIM])
    summary = sbuf(ctx, "summary", [BATCH, DIM])
    v_inv = sbuf(ctx, "v_inv", [KT, DIM])

    done(pool, pool.memset(ident[:, :], 0.0))
    done(pool, pool.affine_select(out=ident[:, :], in_=ident[:, :], compare_op=ALU.not_equal, fill=1.0,
                                  base=0, pattern=[[-1, P]], channel_multiplier=1))
    pool.sem_inc(pair[pool, dve], 1)
    take(dve, pair[pool, dve])
    hand(dve.tensor_copy(ident_b[:, :], ident[:, :]), dve, pe)
    fetched(dve, sp.dma_start(resid[:, :, :], token_tiles(t["x"])))

    def layer_norm(st, x, h, tag):
        stats = sbuf(st, "ln_stats" + tag, [TT, NTT, 6])
        mv = sbuf(st, "ln_mv" + tag, [TT, NTT, 2])
        std = sbuf(st, "ln_std" + tag, [TT, NTT])
        for i in range(NTT):
            last = dve.bn_stats(stats[:, i, :], x[:, i, :])
        done(dve, last)
        for i in range(NTT):
            last = dve.bn_aggr(mv[:, i, :], stats[:, i, :])
        done(dve, last)
        hand(dve.tensor_scalar(std[:, :], mv[:, :, 1], EPS, None, ALU.add), dve, act)
        hand(act.activation(std[:, :], std[:, :], ACT.Sqrt), act, dve)
        done(dve, dve.reciprocal(std[:, :], std[:, :]))
        for i in range(NTT):
            last = dve.tensor_scalar(h[:, i, :], x[:, i, :], mv[:, i, 0:1], std[:, i:i + 1],
                                     ALU.subtract, ALU.mult)
        return last

    def transpose_tokens(h, hT, ps):
        for c in range(NC):
            for i in range(NTT):
                last = pe.transpose(ps[:, 2 * c + i // TPH, (i % TPH) * TT:(i % TPH + 1) * TT],
                                    h[:, i, c * P:(c + 1) * P], ident[0:TT, 0:TT])
        hand(last, pe, dve)
        for c in range(NC):
            last = dve.tensor_copy(hT[:, c, :].rearrange("p (b n) -> p b n", b=2), ps[:, 2 * c:2 * c + 2, 0:HALF])
        return last

    def project_tokens(hT, w, ps, width=DIM):
        for i in range(NTT):
            for c in range(NC):
                last = pe.matmul(ps[:, i, 0:width], hT[:, c, i * TT:(i + 1) * TT], w[:, c, 0:width],
                                 start=(c == 0), stop=(c == NC - 1))
        return last

    def quantise(x, amax, scale, groups):
        xg = x.rearrange("p (g d) -> p g d", d=HDIM)
        n = xg.shape[0]
        sb_ = scale.rearrange("p (g o) -> p g o", o=1).to_broadcast([n, groups, HDIM])
        done(dve, dve.tensor_reduce(amax, xg, axis=AX.X, op=ALU.max, apply_absolute_value=True))
        done(dve, dve.tensor_scalar(scale, amax, 1.0 / QMAX, TINY, ALU.mult, ALU.max))
        done(dve, dve.reciprocal(amax, scale))
        done(dve, dve.tensor_tensor(xg, xg, amax.rearrange("p (g o) -> p g o", o=1).to_broadcast([n, groups, HDIM]),
                                    ALU.mult))
        done(dve, dve.tensor_scalar(x, x, ROUND, ROUND, ALU.add, ALU.subtract))
        return xg, sb_

    with ExitStack() as st:
        h = sbuf(st, "h", [TT, NTT, DIM])
        hT = sbuf(st, "hT", [P, NC, TOK])
        wq = sbuf(st, "wq", [P, NC, DIM])
        bq = sbuf(st, "bq", [TT, DIM])
        q = sbuf(st, "q", [TT, NTT, DIM])
        rest = sbuf(st, "q_rest", [TT, NTT, DIM])
        amax = sbuf(st, "q_amax", [TT, NTT * HEADS])
        scale = sbuf(st, "q_scale", [TT, NTT * HEADS])
        parts = sbuf(st, "q_parts", [TT, NTT, HEADS, KROWS], bf16)
        rows = sbuf(st, "q_rows_sb", [KROWS, HEADS, TOK], bf16)
        ps = psum(st, "ps_q", [P, 4, BANK])
        psp = ps[0:TT, :, :].rearrange("p b (i n) -> p (b i) n", n=DIM)
        psr = [psum(st, f"ps_qrows{i}", [KROWS, 2 * BANK], bf16) for i in range(4)]
        fetched(pe, sp.dma_start(wq[:, :, :], t["L0_xattn_Wq"].rearrange("(c p) n -> p c n", p=P)))
        fetched(dve, sp.dma_start(bq[:, :], bcast(t["L0_xattn_bq"], TT)))
        hand(layer_norm(st, resid, h, "q"), dve, pe)
        hand(transpose_tokens(h, hT, ps), dve, pe)
        hand(project_tokens(hT, wq, psp), pe, dve)
        done(dve, dve.tensor_tensor(q[:, :, :], psp, bq[:, :].rearrange("p (o n) -> p o n", o=1)
                                    .to_broadcast([TT, NTT, DIM]), ALU.add))
        flat = q[:, :, :].rearrange("p t n -> p (t n)")
        done(dve, dve.tensor_scalar(flat, flat, 1.0 / math.sqrt(HDIM), None, ALU.mult))
        xg, sb_ = quantise(flat, amax[:, :], scale[:, :], NTT * HEADS)
        done(dve, dve.tensor_tensor(xg, xg, sb_, ALU.mult))
        qh = q[:, :, :].rearrange("p t (h d) -> p t h d", d=HDIM)
        rh = rest[:, :, :].rearrange("p t (h d) -> p t h d", d=HDIM)

        def part(i):
            return parts[:, :, :, i * HDIM:(i + 1) * HDIM]

        def per_tile(fn):
            for i in range(NTT):
                last = fn(i)
            done(dve, last)
        per_tile(lambda i: dve.tensor_copy(part(0)[:, i], qh[:, i]))
        per_tile(lambda i: dve.tensor_tensor(rh[:, i], qh[:, i], part(0)[:, i], ALU.subtract))
        per_tile(lambda i: dve.tensor_copy(part(3)[:, i], rh[:, i]))
        per_tile(lambda i: dve.tensor_tensor(part(5)[:, i], rh[:, i], part(3)[:, i], ALU.subtract))
        per_tile(lambda i: dve.tensor_copy(part(1)[:, i], part(0)[:, i]))
        per_tile(lambda i: dve.tensor_copy(part(2)[:, i], part(0)[:, i]))
        for i in range(NTT):
            last = dve.tensor_copy(part(4)[:, i], part(3)[:, i])
        hand(last, dve, pe)
        for hd in range(HEADS):
            dst = psr[hd % 4]
            if hd >= 4:
                take(pe, pair[dve, pe])
            for i in range(NTT):
                last = pe.transpose(dst[:, i * TT:(i + 1) * TT], parts[:, i, hd, :], ident_b[0:TT, 0:TT])
            hand(last, pe, dve)
            copied = dve.tensor_copy(rows[:, hd, :], dst[:, 0:TOK])
            if hd < HEADS - 1:
                copied.then_inc(pair[dve, pe], 1)
        take(pe, pair[dve, pe], 3)
        hand(copied, dve, sp)
        fetched(sp, sp.dma_start(q_rows.rearrange("(h r) n -> r h n", r=KROWS), rows[:, :, :]))
    nc.all_engine_barrier()

    ctxT = t["ctxT"].rearrange("(c p) n -> p c n", p=P)
    BLK = 2 * HROWS
    NBLK = HEADS * HROWS // BLK
    with ExitStack() as st:
        wkv = sbuf(st, "wkv", [P, NC, 2 * DIM])
        bkv = sbuf(st, "bkv", [KT, 2 * DIM])
        cx = [sbuf(st, f"cx{u}", [P, NC, GK]) for u in range(2)]
        kv = [sbuf(st, f"kv{u}", [KT, GEN, 2 * DIM]) for u in range(2)]
        kq = [sbuf(st, f"kq{u}", [KT, GEN, DIM]) for u in range(2)]
        rest = [sbuf(st, f"krest{u}", [KT, GEN, DIM]) for u in range(2)]
        kr = sbuf(st, "k_round", [KT, GEN * DIM])
        amax = sbuf(st, "k_amax", [KT, GEN * HEADS])
        scale = sbuf(st, "k_scale", [KT, GEN * HEADS])
        parts = [sbuf(st, f"kparts{u}", [KT, GEN, HEADS, HROWS], bf16) for u in range(2)]
        rows = [sbuf(st, f"krows{u}", [BLK, NBLK, GK], bf16) for u in range(2)]
        v_top = sbuf(st, "v_top", [KT, DIM])
        v_amax = sbuf(st, "v_amax", [KT, DIM])
        v_all = sbuf(st, "v_all", [KT, DIM])
        psk = psum(st, "ps_kv", [KT, GEN, BANK])
        pst = psum(st, "ps_krows", [BLK, NBLK, GEN, P], bf16)
        cx_ld = [semaphore(f"cx_ld{u}") for u in range(2)]
        cx_free = [semaphore(f"cx_free{u}") for u in range(2)]
        kv_ready, kv_bank_free = semaphore("kv_ready"), semaphore("kv_bank_free")
        v_ready, v_out = semaphore("v_ready"), [semaphore(f"v_out{u}") for u in range(2)]
        kq_ready, kq_free = semaphore("kq_ready"), semaphore("kq_free")
        high_ready, rest_ready = semaphore("high_ready"), semaphore("rest_ready")
        mid_ready, low_ready = semaphore("mid_ready"), semaphore("low_ready")
        rows_ready, rows_free = semaphore("rows_ready"), semaphore("rows_free")
        rows_out = [semaphore(f"rows_out{u}") for u in range(2)]

        fetched(pe, sp.dma_start(wkv[:, :, :], t["L0_xattn_Wkv"].rearrange("(c p) n -> p c n", p=P)))
        fetched(dve, sp.dma_start(bkv[:, :], bcast(t["L0_xattn_bkv"], KT)))
        done(dve, dve.memset(v_amax[:, :], 0.0))
        for u in range(2):
            sp.sem_inc(v_out[u], 16)
            act.sem_inc(rows_out[u], 16)
        dve.sem_inc(kv_bank_free, GEN)
        pool.sem_inc(kq_free, 2)
        act.sem_inc(rows_free, 1)

        def load_ctx(n, u):
            sp.dma_start(cx[u][:, :, :], ctxT[:, :, bass.ds(n * GK, GK)]).then_inc(cx_ld[u], 16)

        def project(u):
            take(pe, cx_ld[u], 16)
            for i in range(GEN):
                take(pe, kv_bank_free)
                for c in range(NC):
                    last = pe.matmul(psk[:, i, :], cx[u][:, c, i * KT:(i + 1) * KT], wkv[:, c, :],
                                     start=(c == 0), stop=(c == NC - 1))
                last.then_inc(kv_ready, 1)

        def split(n, u):
            take(dve, v_out[u], 16)
            for i in range(GEN):
                take(dve, kv_ready)
                last = dve.tensor_tensor(kv[u][:, i, :], psk[:, i, :], bkv[:, :], ALU.add)
                if i < GEN - 1:
                    last.then_inc(kv_bank_free, 1)
            tell(dve, last, kv_bank_free, cx_free[u], v_ready)
            take(sp, v_ready)
            sp.dma_start(v_raw[bass.ds(n * GEN, GEN), :, :].rearrange("t p d -> p t d"),
                         kv[u][:, :, DIM:]).then_inc(v_out[u], 16)
            kg = kv[u][:, :, 0:DIM].rearrange("p t (h d) -> p t h d", d=HDIM)
            sg = scale[:, :].rearrange("p (t h) -> p t h", t=GEN)
            done(dve, dve.tensor_reduce(amax[:, :].rearrange("p (t h) -> p t h", t=GEN), kg, axis=AX.X,
                                        op=ALU.max, apply_absolute_value=True))
            done(dve, dve.tensor_scalar(scale[:, :], amax[:, :], 1.0 / QMAX, TINY, ALU.mult, ALU.max))
            done(dve, dve.reciprocal(amax[:, :], scale[:, :]))
            s3 = scale[:, :].rearrange("p (g o) -> p g o", o=1).to_broadcast([KT, GEN * HEADS, HDIM])
            k3 = kr[:, :].rearrange("p (g d) -> p g d", d=HDIM)
            s4 = amax[:, :].rearrange("p (t h o) -> p t h o", t=GEN, o=1).to_broadcast([KT, GEN, HEADS, HDIM])
            k4 = kr[:, :].rearrange("p (t h d) -> p t h d", t=GEN, d=HDIM)
            done(dve, dve.tensor_tensor(k4, kg, s4, ALU.mult))
            done(dve, dve.tensor_scalar(kr[:, :], kr[:, :], ROUND, ROUND, ALU.add, ALU.subtract))
            take(dve, kq_free)
            q3 = kq[u][:, :, :].rearrange("p t (h d) -> p (t h) d", d=HDIM)
            dve.tensor_tensor(q3, k3, s3, ALU.mult).then_inc(kq_ready, 1)
            done(dve, dve.tensor_reduce(v_top[:, :], kv[u][:, :, DIM:].rearrange("p t d -> p d t"), axis=AX.X,
                                        op=ALU.max, apply_absolute_value=True))
            done(dve, dve.tensor_tensor(v_amax[:, :], v_amax[:, :], v_top[:, :], ALU.max))

            def part(i):
                return parts[u][:, :, :, i * HDIM:(i + 1) * HDIM].rearrange("p t h d -> p (t h) d")
            r3 = rest[u][:, :, :].rearrange("p t (h d) -> p (t h) d", d=HDIM)
            take(act, kq_ready)
            act.activation(part(0), q3, ACT.Copy).then_inc(high_ready, 1)
            take(pool, high_ready)
            tell(pool, pool.tensor_tensor(r3, q3, part(0), ALU.subtract), rest_ready, kq_free)
            return part, r3

        def split_low(u, part, r3):
            take(act, rest_ready)
            act.activation(part(1), r3, ACT.Copy).then_inc(mid_ready, 1)
            take(pool, mid_ready)
            pool.tensor_tensor(part(2), r3, part(1), ALU.subtract).then_inc(low_ready, 1)

        def transpose_rows(n, u):
            take(pe, low_ready)
            take(pe, rows_free)
            flat = parts[u][:, :, :, :].rearrange("p t h r -> p t (h r)")
            for i in range(GEN):
                for b in range(NBLK):
                    last = pe.transpose(pst[:, b, i, 0:KT], flat[:, i, b * BLK:(b + 1) * BLK], ident_b[0:KT, 0:KT])
            last.then_inc(rows_ready, 1)
            take(act, rows_ready)
            take(act, rows_out[u], 16)
            tell(act, act.activation(rows[u][:, :, :].rearrange("p b (t k) -> p (b t) k", k=KT),
                                     pst[:, :, :, :].rearrange("p b t k -> p (b t) k")[:, :, 0:KT], ACT.Copy),
                 rows_free)
            act.dma_start(k_rows.rearrange("(b p) n -> p b n", p=BLK)[:, :, bass.ds(n * GK, GK)],
                          rows[u][:, :, :]).then_inc(rows_out[u], 16)

        def step(n, u, load, more, before):
            if more:
                project(1 - u)
            part, r3 = split(n, u)
            take(sp, cx_free[u])
            if load:
                load_ctx(n + 2, u)
            if before:
                transpose_rows(n - 1, 1 - u)
            split_low(u, part, r3)

        load_ctx(0, 0)
        load_ctx(1, 1)
        project(0)
        step(0, 0, True, True, False)
        with nc.Fori(0, (NGEN - 4) // 2) as i:
            step(i * 2 + 1, 1, True, True, True)
            step(i * 2 + 2, 0, True, True, True)
        step(NGEN - 3, 1, True, True, True)
        step(NGEN - 2, 0, False, True, True)
        step(NGEN - 1, 1, False, False, True)
        transpose_rows(NGEN - 1, 1)
        for u in range(2):
            take(sp, v_out[u], 16)
            take(act, rows_out[u], 16)
        take(pool, kq_free, 2)
        take(pe, kv_bank_free, GEN)
        take(pe, rows_free)
        done(dve, dve.tensor_copy(v_top[:, :], v_amax[:, :]))
        hand(dve.tensor_copy(v_amax[:, :], v_top[:, :]), dve, pool)
        hand(pool.partition_all_reduce(v_all[:, :], v_amax[:, :], KT, bass.bass_isa.ReduceOp.absmax), pool, dve)
        done(dve, dve.tensor_scalar(v_scale[:, :], v_all[:, :], 1.0 / QMAX, TINY, ALU.mult, ALU.max))
        done(dve, dve.reciprocal(v_inv[:, :], v_scale[:, :]))
    nc.all_engine_barrier()

    with ExitStack() as st:
        vf = [sbuf(st, f"vf{u}", [KT, CT, DIM]) for u in range(2)]
        vq = [sbuf(st, f"vq{u}", [KT, HEADS, CT, HDIM], bf16) for u in range(2)]
        vf_ld = [semaphore(f"vf_ld{u}") for u in range(2)]
        vf_free = [semaphore(f"vf_free{u}") for u in range(2)]
        vq_ready = semaphore("vq_ready")
        vq_out = [semaphore(f"vq_out{u}") for u in range(2)]
        for u in range(2):
            dve.sem_inc(vq_out[u], 16)
            dve.sem_inc(vf_free[u], 1)

        def quantise_values(j, u):
            take(sp, vf_free[u])
            sp.dma_start(vf[u][:, :, :], v_raw[bass.ds(j * CT, CT), :, :].rearrange("t p d -> p t d"))\
              .then_inc(vf_ld[u], 16)
            take(dve, vf_ld[u], 16)
            done(dve, dve.tensor_tensor(vf[u][:, :, :], vf[u][:, :, :],
                                        v_inv[:, :].rearrange("p (o d) -> p o d", o=1)
                                        .to_broadcast([KT, CT, DIM]), ALU.mult))
            take(dve, vq_out[u], 16)
            tell(dve, dve.tensor_scalar(vq[u][:, :, :, :].rearrange("p h t d -> p t h d"),
                                        vf[u][:, :, :].rearrange("p t (h d) -> p t h d", d=HDIM),
                                        ROUND, ROUND, ALU.add, ALU.subtract), vf_free[u], vq_ready)
            take(act, vq_ready)
            act.dma_start(v_int.rearrange("h j p n -> p h j n")[:, :, bass.ds(j, 1), :],
                          vq[u][:, :, :, :].rearrange("p h t d -> p h (t d)")
                          .rearrange("p h (o n) -> p h o n", o=1)).then_inc(vq_out[u], 16)

        with nc.Fori(0, NCH // 2) as i:
            for u in range(2):
                quantise_values(i * 2 + u, u)
        for u in range(2):
            take(act, vq_out[u], 16)
            take(sp, vf_free[u])
    nc.all_engine_barrier()

    SLOTS = 6
    LAG = 3
    UNITS = NQB * NPIECE
    with ExitStack() as st:
        k1 = [sbuf(st, f"k1_{u}", [KROWS, CK], bf16) for u in range(2)]
        k2 = [sbuf(st, f"k2_{u}", [MROWS, CK], bf16) for u in range(2)]
        q1 = sbuf(st, "q1", [MROWS, TOK], bf16)
        q2 = sbuf(st, "q2", [MROWS, TOK], bf16)
        vt = [sbuf(st, f"vt{u}", [KT, CT, HDIM], bf16) for u in range(2)]
        e = [sbuf(st, f"e{i}", [KT, 2, HALF]) for i in range(SLOTS)]
        r = [sbuf(st, f"r{i}", [KT, 2, HALF], bf16) for i in range(SLOTS)]
        z = [sbuf(st, f"z{i}", [KT, 2, HALF]) for i in range(SLOTS // 2)]
        ones = sbuf(st, "ones", [KT, SUMROWS])
        zeros = sbuf(st, "zeros", [KT, HALF], bf16)
        unit_max = sbuf(st, "unit_max", [QB, NQB, NCH * NPIECE])
        run_max = sbuf(st, "run_max", [QB, NQB])
        shift = sbuf(st, "shift", [QB, NQB])
        shift_parts = sbuf(st, "shift_parts", [QB, NQB, PARTS], bf16)
        av = sbuf(st, "av", [P, HALF])
        inv_z = sbuf(st, "inv_z", [TT, TPH, 2])
        head_out = sbuf(st, "head_out", [TT, NTT, HDIM])
        decay = sbuf(st, "decay", [P, 1])
        keep = sbuf(st, "keep", [P, LCTX])
        ones_c = sbuf(st, "ones_c", [P, LCTX])
        weight = sbuf(st, "weight", [P, LCTX])
        wsum = sbuf(st, "wsum", [P, 1])
        cb = [sbuf(st, f"cb{u}", [P, NC, LCTX]) for u in range(2)]
        prod = sbuf(st, "prod", [P, LCTX])
        csum = sbuf(st, "csum", [P, NC])
        ctx_sum = sbuf(st, "ctx_sum", [P, NC, BATCH])
        cb_ld, cb_free = ([semaphore(f"{n}{u}") for u in range(2)] for n in ("cb_ld", "cb_free"))

        ps1 = [psum(st, f"ps_sweep1_{i}", [P, 2, BANK]) for i in range(2)]
        ps2 = [psum(st, f"ps_sweep2_{i}", [KT, BANK]) for i in range(3)]
        psav = psum(st, "ps_av", [P, BANK])
        k1_ld, k1_free, k2_ld, k2_free, v_ld, v_free = (
            [semaphore(f"{n}{u}") for u in range(2)]
            for n in ("k1_ld", "k1_free", "k2_ld", "k2_free", "v_ld", "v_free"))
        s2_ready, s2_free, e_free, s1_ready, s1_free, q1_free, q1_ld, head_stored = (
            semaphore(n) for n in ("s2_ready", "s2_free", "e_free", "s1_ready", "s1_free",
                                   "q1_free", "q1_ld", "head_stored"))
        e_ready, r_ready, pair_ready, z_ready = (semaphore(n) for n in ("e_ready", "r_ready", "pair_ready", "z_ready"))

        done(pool, pool.memset(zeros[:, :], 0.0))
        for u in range(2):
            done(pool, pool.memset(k2[u][KROWS:MROWS, :], 1.0))
        hand(pool.memset(ones[:, :], 1.0), pool, pe)
        for u in range(2):
            dve.sem_inc(k1_free[u], 1)
            dve.sem_inc(k2_free[u], 1)
            dve.sem_inc(v_free[u], 1)
            dve.sem_inc(cb_free[u], 1)
        dve.sem_inc(s2_free, 3)
        dve.sem_inc(s1_free, 2)
        dve.sem_inc(e_free, SLOTS)
        dve.sem_inc(head_stored, 16)

        done(dve, dve.memset(ones_c[:, :], 1.0))
        fetched(act, sp.dma_start(decay[:, :], bcast(t["L1_xattn_decay"], P)))
        hand(act.activation(decay[:, :], decay[:, :], ACT.Sigmoid), act, dve)
        done(dve, dve.tensor_scalar(keep[:, :], ones_c[:, :], decay[:, 0:1], None, ALU.mult))
        done(dve, dve.tensor_tensor_scan(weight[:, :], keep[:, :], ones_c[:, :], 0.0, ALU.mult, ALU.add))
        done(dve, dve.tensor_reduce(wsum[:, :], weight[:, :], axis=AX.X, op=ALU.add))
        done(dve, dve.tensor_copy(keep[:, :], weight[:, ::-1]))

        def weigh_context(b, u):
            take(sp, cb_free[u])
            sp.dma_start(cb[u][:, :, :], ctxT[:, :, bass.ds(b * LCTX, LCTX)]).then_inc(cb_ld[u], 16)
            take(dve, cb_ld[u], 16)
            for c in range(NC):
                done(dve, dve.tensor_tensor_reduce(out=prod[:, :], in0=cb[u][:, c, :], in1=keep[:, :], scale=1.0,
                                                   scalar=0.0, op0=ALU.mult, op1=ALU.add,
                                                   accum_out=csum[:, c:c + 1]))
            dve.sem_inc(cb_free[u], 1)
            done(dve, dve.tensor_copy(ctx_sum[:, :, bass.ds(b, 1)], csum[:, :].rearrange("p (c o) -> p c o", o=1)))

        def load_keys(dst, sem, head, j):
            at = head * HROWS
            for lo, n in ((0, HROWS), (HROWS, 2 * HDIM), (HROWS + 2 * HDIM, HDIM)):
                sp.dma_start(dst[lo:lo + n, :], k_rows[bass.ds(at, n), bass.ds(j * CK, CK)]).then_inc(sem, 16)

        def load_first(head, j, u):
            take(sp, k1_free[u])
            load_keys(k1[u], k1_ld[u], head, j)

        def load_second(head, j, u):
            take(sp, k2_free[u])
            load_keys(k2[u], k2_ld[u], head, j)
            take(sp, v_free[u])
            sp.dma_start(vt[u][:, :, :].rearrange("p t d -> p (t d)"),
                         v_int[bass.ds(head, 1), bass.ds(j, 1), :, :].rearrange("h j p n -> (h j p) n"))\
              .then_inc(v_ld[u], 16)

        def scores(i, u):
            if i == 0:
                take(pe, k2_ld[u], 48)
            for g in range(2):
                ps = ps2[(2 * i + g) % 3]
                take(pe, s2_free)
                pe.matmul(ps[:, 0:HALF], k2[u][:, i * KT:(i + 1) * KT], q2[:, g * HALF:(g + 1) * HALF],
                          start=True, stop=True).then_inc(s2_ready, 1)
                if i % 2 == 0 and g == 0:
                    take(act, e_free, 2)
                take(act, s2_ready)
                exp = act.activation(e[i % SLOTS][:, g, :], ps[:, 0:HALF], ACT.Exp)
                if g == 0:
                    exp.then_inc(s2_free, 1)
                else:
                    tell(act, exp, s2_free, e_ready, *([pair_ready] if i % 2 else []))

        def rounded(i, u):
            es = e[i % SLOTS][:, :, :]
            take(dve, e_ready)
            if i == CT - 1:
                dve.sem_inc(k2_free[u], 1)
            dve.tensor_scalar(r[i % SLOTS][:, :, :], es, ROUND, ROUND, ALU.add, ALU.subtract).then_inc(r_ready, 1)
            if i % 2:
                take(pool, pair_ready)
                pool.tensor_tensor(z[i // 2 % (SLOTS // 2)][:, :, :], e[(i - 1) % SLOTS][:, :, :], es, ALU.add)\
                    .then_inc(z_ready, 1)

        def unit(n, u, j, head_start):
            piece, b = divmod(n, NQB)
            ps = ps1[(n + u) % 2]
            if n == 0:
                take(pe, k1_ld[u], 48)
                if head_start:
                    take(pe, q1_ld, 16)
            take(pe, s1_free)
            for i in range(2):
                at = (piece * 2 + i) * SB
                last = pe.matmul(ps[:, i, 0:SB], q1[0:KROWS, b * QB:(b + 1) * QB], k1[u][:, at:at + SB],
                                 start=True, stop=True)
            last.then_inc(s1_ready, 1)
            take(dve, s1_ready)
            top = dve.tensor_reduce(unit_max[:, b, bass.ds(j * NPIECE + piece, 1)], ps[:, :, 0:SB], axis=AX.XY,
                                    op=ALU.max)
            if n < UNITS - 1:
                top.then_inc(s1_free, 1)
            else:
                tell(dve, top, s1_free, k1_free[u])

        def sums(i, u, head_end=False):
            s = i % SLOTS
            if i == 0:
                take(pe, v_ld[u], 16)
            take(pe, r_ready)
            for g in range(2):
                c = g * SUMROWS
                last = pe.matmul(psav[c:c + HDIM, 0:HALF], vt[u][:, i, :], r[s][:, g, :],
                                 start=False, stop=False, skip_group_check=True, tile_position=(0, c))
            if i == CT - 1:
                last.then_inc(v_free[u], 1)
            if i % 2 == 0:
                return
            take(pe, z_ready)
            for g in range(2):
                c = (2 + g) * SUMROWS
                last = pe.matmul(psav[c:c + SUMROWS, 0:HALF], ones[:, :], z[i // 2 % (SLOTS // 2)][:, g, :],
                                 start=False, stop=False, skip_group_check=True, tile_position=(0, c))
            if head_end:
                done(pe, last)
                pe.sem_inc(e_free, 2)
                pe.sem_inc(pair[pe, act], 1)
            else:
                last.then_inc(e_free, 2)

        def chunk(first, second, j, u, at=0, head_start=False, last=False):
            n = 0
            for i in range(at, CT):
                if second:
                    scores(i, u)
                    rounded(i, u)
                left = CT - i - (LAG if last else 0)
                if first and n < UNITS and (left <= UNITS - n or i % 8 != 7):
                    unit(n, u, j, head_start)
                    n += 1
                if first and last and i == CT - LAG:
                    shifts()
                if first and last and i == CT - LAG + 1:
                    shift_rows()
                if second and i >= LAG:
                    sums(i - LAG, u)
                elif second:
                    sums(i - LAG + CT, 1 - u)

        def shifts():
            done(dve, dve.tensor_reduce(run_max[:, :], unit_max[:, :, :], axis=AX.X, op=ALU.max))
            done(dve, dve.tensor_scalar(shift[:, :], run_max[:, :], -1.0, LOG255, ALU.mult, ALU.add))
            done(dve, dve.tensor_copy(shift_parts[:, :, 0], shift[:, :]))
            done(dve, dve.tensor_tensor(shift[:, :], shift[:, :], shift_parts[:, :, 0], ALU.subtract))
            done(dve, dve.tensor_copy(shift_parts[:, :, 1], shift[:, :]))
            dve.tensor_tensor(shift_parts[:, :, 2], shift[:, :], shift_parts[:, :, 1], ALU.subtract)\
               .then_inc(pair[dve, pe], 1)

        def shift_rows():
            take(pe, pair[dve, pe])
            take(pe, s1_free, 2)
            for b in range(NQB):
                last = pe.matmul(ps1[0][KROWS:MROWS, b // 4, (b % 4) * QB:(b % 4 + 1) * QB], shift_parts[:, b, :],
                                 ident_b[:, :], start=True, stop=True, tile_position=(0, KROWS))
            hand(last, pe, dve)
            dve.tensor_copy(q1[KROWS:MROWS, 0:BANK], ps1[0][KROWS:MROWS, 0, :])
            tell(dve, dve.tensor_copy(q1[KROWS:MROWS, BANK:TOK], ps1[0][KROWS:MROWS, 1, 0:TOK - BANK]), s1_free)

        def start_second_sweep(head):
            load_second(head, 0, 0)
            tell(dve, dve.tensor_copy(q2[:, :], q1[:, :]), pair[dve, pe], q1_free)
            take(pe, pair[dve, pe])

        def first_tiles(after_head):
            for i in range(LAG):
                scores(i, 0)
                rounded(i, 0)
                if after_head:
                    sums(i - LAG + CT, 1, head_end=(i == LAG - 1))

        def clear_sums():
            for g in range(4):
                pe.matmul(psav[g * SUMROWS:(g + 1) * SUMROWS, 0:HALF], zeros[:, 0:SUMROWS], zeros[:, :],
                          start=True, stop=True, tile_position=(0, g * SUMROWS))

        def finish_head(head):
            take(act, pair[pe, act])
            hand(act.activation(av[:, :], psav[:, 0:HALF], ACT.Copy), act, pe)
            clear_sums()
            for i in range(TPH):
                last = pe.transpose(ps1[1][0:TT, 0, i * P:(i + 1) * P], av[:, i * TT:(i + 1) * TT], ident[:, :])
            hand(last, pe, dve)
            tr = ps1[1][0:TT, 0, :].rearrange("p (i g c) -> p i g c", i=TPH, c=SUMROWS)
            done(dve, dve.reciprocal(inv_z[:, :, :], tr[:, :, 2:4, 0]))
            take(dve, head_stored, 16)
            for g in range(2):
                last = dve.tensor_tensor(head_out[:, g * TPH:(g + 1) * TPH, :], tr[:, :, g, 0:HDIM],
                                         inv_z[:, :, g:g + 1].to_broadcast([TT, TPH, HDIM]), ALU.mult)
            tell(dve, last, pair[dve, act], s1_free)
            take(act, pair[dve, act])
            act.dma_start(token_tiles(attn_rows)[:, :, bass.ds(head * HDIM, HDIM)],
                         head_out[:, :, :]).then_inc(head_stored, 16)

        def sweep(h1, h2, beside=None):
            def load(j, u):
                if h1 is not None:
                    load_first(h1, j, u)
                if h2 is not None:
                    load_second(h2, j, u)

            def steps(j, u, **kw):
                chunk(h1 is not None, h2 is not None, j, u, **kw)
                if beside is not None:
                    beside(j)
            if h1 is not None:
                load_first(h1, 0, 0)
                take(sp, q1_free)
                sp.dma_start(q1[0:KROWS, :], q_rows[bass.ds(h1 * KROWS, KROWS), :]).then_inc(q1_ld, 16)
            steps(0, 0, at=0 if h2 is None else LAG, head_start=True)
            with nc.Fori(0, (NCH - 2) // 2) as jj:
                for u in (1, 0):
                    load(jj * 2 + 2 - u, u)
                    steps(jj * 2 + 2 - u, u)
            load(NCH - 1, 1)
            steps(NCH - 1, 1, last=True)

        dve.sem_inc(q1_free, 1)
        sweep(0, None)
        start_second_sweep(0)
        first_tiles(False)
        pe.sem_inc(s1_free, 1)
        clear_sums()
        with nc.Fori(0, HEADS - 1) as hd:
            sweep(hd + 1, hd)
            start_second_sweep(hd + 1)
            first_tiles(True)
            finish_head(hd)

        def weigh_two(j):
            weigh_context(j * 2, 0)
            weigh_context(j * 2 + 1, 1)

        sweep(None, HEADS - 1, weigh_two)
        for i in range(CT - LAG, CT):
            sums(i, 1, head_end=(i == CT - 1))
        take(pe, s1_free, 2)
        finish_head(HEADS - 1)
        take(act, head_stored, 16)
        take(sp, q1_free)
        for u in range(2):
            take(sp, k1_free[u])
            take(sp, k2_free[u])
            take(sp, v_free[u])
            take(sp, cb_free[u])
        take(pe, s2_free, 3)
        take(pe, s1_free)
        take(act, e_free, SLOTS)
        nc.all_engine_barrier()

        w_in = sbuf(st, "w_in", [P, NC, DIM])
        w_out = sbuf(st, "w_out", [P, NC, DIM])
        b_in = sbuf(st, "b_in", [P, NC])
        b_out = sbuf(st, "b_out", [BATCH, DIM])
        mean = sbuf(st, "mean_state", [P, NC, BATCH])
        with nc.allow_non_contiguous_dma(reason="a bias as columns, once"):
            fetched(dve, sp.dma_start(b_in[:, :], t["L1_xattn_b_in"].rearrange("(c p) -> p c", p=P)),
                    sp.dma_start(b_out[:, :], bcast(t["L1_xattn_b_out"], BATCH)))
        fetched(pe, sp.dma_start(w_in[:, :, :], t["W_inT"].rearrange("(c p) n -> p c n", p=P)),
                sp.dma_start(w_out[:, :, :], t["W_outT"].rearrange("(c p) n -> p c n", p=P)))
        hand(dve.tensor_scalar(b_in[:, :], b_in[:, :], wsum[:, 0:1], None, ALU.mult), dve, pe)
        for m in range(NC):
            for c in range(NC):
                last = pe.matmul(ps1[0][:, m, 0:BATCH], w_in[:, c, m * P:(m + 1) * P], ctx_sum[:, c, :],
                                 start=(c == 0), stop=(c == NC - 1))
        hand(last, pe, dve)
        for m in range(NC):
            last = dve.tensor_scalar(mean[:, m, :], ps1[0][:, m, 0:BATCH], b_in[:, m:m + 1], 1.0 / LCTX,
                                     ALU.add, ALU.mult)
        hand(last, dve, pe)
        for c in range(NC):
            last = pe.matmul(ps1[1][0:BATCH, 0, 0:DIM], mean[:, c, :], w_out[:, c, :],
                             start=(c == 0), stop=(c == NC - 1))
        hand(last, pe, dve)
        done(dve, dve.tensor_tensor(summary[:, :], ps1[1][0:BATCH, 0, 0:DIM], b_out[:, :], ALU.add))
    nc.all_engine_barrier()

    def experts(st, tag, hT, comb, acc, n_exp, f, w_gu, w_dn):
        gu_w = [sbuf(st, f"gu_w{tag}{u}", [P, NC, 2 * f]) for u in range(2)]
        dn_w = [sbuf(st, f"dn_w{tag}{u}", [f, DIM]) for u in range(2)]
        gate = sbuf(st, "gate" + tag, [f, 2, HALF])
        hid = [sbuf(st, f"hid{tag}{u}", [f, 2, HALF]) for u in range(2)]
        cw = sbuf(st, "cw" + tag, [TT, NTT, 1])
        psg = psum(st, "ps_gate" + tag, [f, 2, BANK])
        psu = psum(st, "ps_up" + tag, [f, 2, BANK])
        psd = psum(st, "ps_down" + tag, [TT, NTT, DIM])
        gu_ld, gu_free, dn_ld, dn_free = (
            [semaphore(f"{n}{tag}{u}") for u in range(2)] for n in ("gu_ld", "gu_free", "dn_ld", "dn_free"))
        gu_ready, up_free, gate_ready, hid_ready, dn_ready, dn_read = (
            semaphore(n + tag) for n in ("gu_ready", "up_free", "gate_ready", "hid_ready", "dn_ready", "dn_read"))
        dve.sem_inc(up_free, 1)
        dve.sem_inc(dn_read, 1)

        def load_gu(x, u):
            sp.dma_start(gu_w[u][:, :, :].rearrange("p c n -> p (c n)"),
                         w_gu[bass.ds(x, 1), :, :].rearrange("e p n -> (e p) n")).then_inc(gu_ld[u], 16)

        def load_dn(x, u):
            sp.dma_start(dn_w[u][:, :], w_dn[bass.ds(x, 1), :, :].rearrange("e p n -> (e p) n"))\
              .then_inc(dn_ld[u], 16)

        def hidden(x, u, ahead):
            take(pe, gu_ld[u], 16)
            take(pe, up_free)
            for ps, lo in ((psg, 0), (psu, f)):
                for g in range(2):
                    for c in range(NC):
                        last = pe.matmul(ps[:, g, 0:HALF], gu_w[u][:, c, lo:lo + f],
                                         hT[:, c, g * HALF:(g + 1) * HALF], start=(c == 0), stop=(c == NC - 1))
            last.then_inc(gu_ready, 1)
            take(act, gu_ready)
            act.activation(gate[:, :, :], psg[:, :, 0:HALF], ACT.Silu).then_inc(gate_ready, 1)
            take(dve, gate_ready)
            tell(dve, dve.tensor_tensor(hid[u][:, :, :], psu[:, :, 0:HALF], gate[:, :, :], ALU.mult),
                 hid_ready, up_free, gu_free[u])
            take(sp, gu_free[u])
            if ahead:
                load_gu(x + 2, u)

        def step(x, u, left=0):
            if left != 1:
                hidden(x + 1, 1 - u, left not in (2, 3))
            take(pe, dn_ld[u], 16)
            take(pe, hid_ready)
            take(pe, dn_read)
            for i in range(NTT):
                last = pe.matmul(psd[:, i, :], hid[u][:, i // TPH, (i % TPH) * TT:(i % TPH + 1) * TT], dn_w[u][:, :],
                                 start=True, stop=True)
            last.then_inc(dn_ready, 1)
            done(dve, dve.tensor_copy(cw[:, :, :], comb[:, :, bass.ds(x, 1)]))
            take(dve, dn_ready)
            for i in range(NTT):
                last = dve.scalar_tensor_tensor(acc[:, i, :], psd[:, i, :], cw[:, i, :], acc[:, i, :],
                                                ALU.mult, ALU.add)
            tell(dve, last, dn_read, dn_free[u])
            take(sp, dn_free[u])
            if left not in (1, 2):
                load_dn(x + 2, u)

        for u in range(2):
            load_gu(u, u)
            load_dn(u, u)
        hidden(0, 0, True)
        with nc.Fori(0, (n_exp - 4) // 2) as i:
            for u in range(2):
                step(i * 2 + u, u)
        for left in (4, 3, 2, 1):
            step(n_exp - left, left % 2, left)
        take(pe, up_free)
        take(pe, dn_read)

    def top_mask(st, tag, vals, mask, n, k, pad):
        top = sbuf(st, "top" + tag, [TT, NTT, 8])
        marked = sbuf(st, "marked" + tag, [TT, NTT, n + pad])
        for i in range(NTT):
            last = dve.max(top[:, i, :], vals[:, i, :])
        done(dve, last)
        for i in range(NTT):
            last = dve.match_replace(out=marked[:, i, :], in_to_replace=top[:, i, :], in_values=vals[:, i, :],
                                     imm_value=-3.0e38)
        done(dve, last)
        done(dve, dve.tensor_tensor(mask[:, :, :], marked[:, :, pad:], vals[:, :, pad:], ALU.not_equal))
        return top

    PAD0, PAD1 = 8 - N_SEL0, 8 - N_SEL1
    with ExitStack() as st:
        h = sbuf(st, "h0", [TT, NTT, DIM])
        hT = sbuf(st, "hT0", [P, NC, TOK])
        comb = sbuf(st, "comb0", [TT, NTT, N_ALL0])
        with ExitStack() as s2:
            wp = sbuf(s2, "wp", [P, NC, DIM])
            gw = sbuf(s2, "gate_w", [P, NC, N_EXP0])
            bp = sbuf(s2, "bp", [TT, DIM])
            score = sbuf(s2, "score", [TT, NTT, N_EXP0 + PAD0])
            mask = sbuf(s2, "mask0", [TT, NTT, N_EXP0])
            total = sbuf(s2, "total0", [TT, NTT])
            ps = psum(s2, "ps_a", [P, 4, BANK])
            psb = psum(s2, "ps_b", [P, 4, BANK])
            psp = psb[0:TT, :, :].rearrange("p b (i n) -> p (b i) n", n=DIM)
            fetched(pe, sp.dma_start(wp[:, :, :], t["L0_xattn_Wp"].rearrange("(c p) n -> p c n", p=P)),
                    sp.dma_start(gw[:, :, :], t["L0_ffn_gate_w"].rearrange("(c p) n -> p c n", p=P)))
            fetched(dve, sp.dma_start(bp[:, :], bcast(t["L0_xattn_bp"], TT)),
                    sp.dma_start(h[:, :, :], token_tiles(attn_rows)))
            hand(dve.tensor_tensor(h[:, :, :], h[:, :, :], v_scale[0:TT, :].rearrange("p (o d) -> p o d", o=1)
                                   .to_broadcast([TT, NTT, DIM]), ALU.mult), dve, pe)
            hand(transpose_tokens(h, hT, ps), dve, pe)
            hand(project_tokens(hT, wp, psp), pe, dve)
            done(dve, dve.tensor_tensor(resid[:, :, :], resid[:, :, :], psp, ALU.add))
            done(dve, dve.tensor_tensor(resid[:, :, :], resid[:, :, :], bp[:, :].rearrange("p (o d) -> p o d", o=1)
                                        .to_broadcast([TT, NTT, DIM]), ALU.add))
            hand(layer_norm(s2, resid, h, "0"), dve, pe)
            hand(transpose_tokens(h, hT, ps), dve, pe)
            hand(project_tokens(hT, gw, psp, N_EXP0), pe, act)
            hand(dve.memset(score[:, :, 0:PAD0], 3.0), dve, act)
            hand(act.activation(score[:, :, PAD0:], psp[:, :, 0:N_EXP0], ACT.Sigmoid), act, dve)
            top_mask(s2, "0", score, mask, N_EXP0, N_SEL0, PAD0)
            done(dve, dve.tensor_tensor(mask[:, :, :], mask[:, :, :], score[:, :, PAD0:], ALU.mult))
            done(dve, dve.tensor_reduce(total[:, :], mask[:, :, :], axis=AX.X, op=ALU.add))
            done(dve, dve.tensor_scalar(total[:, :], total[:, :], 1e-20, None, ALU.add))
            done(dve, dve.reciprocal(total[:, :], total[:, :]))
            done(dve, dve.tensor_tensor(comb[:, :, 0:N_EXP0], mask[:, :, :],
                                        total[:, :].rearrange("p (t o) -> p t o", o=1)
                                        .to_broadcast([TT, NTT, N_EXP0]), ALU.mult))
            done(dve, dve.memset(comb[:, :, N_EXP0:], 1.0))
        nc.all_engine_barrier()
        experts(st, "0", hT, comb, resid, N_ALL0, F0, t["gu0"], t["dn0"])
    nc.all_engine_barrier()

    with ExitStack() as st:
        h = sbuf(st, "h1", [TT, NTT, DIM])
        hT = sbuf(st, "hT1", [P, NC, TOK])
        comb = sbuf(st, "comb1", [TT, NTT, N_ALL1])
        with ExitStack() as s2:
            sel = sbuf(s2, "sel", [BATCH, TOK])
            z = sbuf(s2, "z", [TT, NTT, DIM])
            gamma = sbuf(s2, "gamma", [TT, DIM])
            beta = sbuf(s2, "beta", [TT, DIM])
            rw = sbuf(s2, "router_w", [P, NC, N_EXP1])
            logit = sbuf(s2, "logit", [TT, NTT, N_EXP1 + PAD1])
            diff = sbuf(s2, "diff", [TT, NTT, N_EXP1])
            mask = sbuf(s2, "mask1", [TT, NTT, N_EXP1])
            total = sbuf(s2, "total1", [TT, NTT])
            ps = psum(s2, "ps_c", [P, 4, BANK])
            psb = psum(s2, "ps_d", [P, 4, BANK])
            psp = psb[0:TT, :, :].rearrange("p b (i n) -> p (b i) n", n=DIM)

            def over_tokens(v):
                return v[:, :].rearrange("p (o d) -> p o d", o=1).to_broadcast([TT, NTT, DIM])
            fetched(pe, sp.dma_start(rw[:, :, :], t["router_wT"].rearrange("(c p) n -> p c n", p=P)))
            fetched(dve, sp.dma_start(gamma[:, :], bcast(t["L1_xattn_gamma"], TT)),
                    sp.dma_start(beta[:, :], bcast(t["L1_xattn_beta"], TT)))
            done(pool, pool.memset(sel[:, :], 1.0))
            done(pool, pool.affine_select(out=sel[:, :], in_=sel[:, :], compare_op=ALU.is_ge, fill=0.0,
                                          base=0, pattern=[[1, TOK]], channel_multiplier=-SEQ))
            hand(pool.affine_select(out=sel[:, :], in_=sel[:, :], compare_op=ALU.is_ge, fill=0.0,
                                    base=SEQ - 1, pattern=[[-1, TOK]], channel_multiplier=SEQ), pool, pe)
            done(dve, layer_norm(s2, resid, z, "z"))
            for i in range(NTT):
                last = pe.matmul(psp[:, i, :], sel[:, i * TT:(i + 1) * TT], summary[:, :], start=True, stop=True)
            hand(last, pe, dve)
            done(dve, dve.tensor_tensor(z[:, :, :], z[:, :, :], psp, ALU.add))
            done(dve, layer_norm(s2, z, h, "y"))
            done(dve, dve.tensor_tensor(h[:, :, :], h[:, :, :], over_tokens(gamma), ALU.mult))
            done(dve, dve.tensor_tensor(h[:, :, :], h[:, :, :], over_tokens(beta), ALU.add))
            done(dve, dve.tensor_tensor(resid[:, :, :], resid[:, :, :], h[:, :, :], ALU.add))
            hand(layer_norm(s2, resid, h, "1"), dve, pe)
            hand(transpose_tokens(h, hT, ps), dve, pe)
            hand(project_tokens(hT, rw, psp, N_EXP1), pe, dve)
            done(dve, dve.memset(logit[:, :, 0:PAD1], 3.0e38))
            done(dve, dve.tensor_copy(logit[:, :, PAD1:], psp[:, :, 0:N_EXP1]))
            top = top_mask(s2, "1", logit, mask, N_EXP1, N_SEL1, PAD1)
            hand(dve.tensor_tensor(diff[:, :, :], logit[:, :, PAD1:],
                                   top[:, :, PAD1:PAD1 + 1].to_broadcast([TT, NTT, N_EXP1]), ALU.subtract), dve, act)
            hand(act.activation(diff[:, :, :], diff[:, :, :], ACT.Exp), act, dve)
            done(dve, dve.tensor_tensor(diff[:, :, :], diff[:, :, :], mask[:, :, :], ALU.mult))
            done(dve, dve.tensor_reduce(total[:, :], diff[:, :, :], axis=AX.X, op=ALU.add))
            done(dve, dve.reciprocal(total[:, :], total[:, :]))
            for half in range(2):
                done(dve, dve.tensor_tensor(comb[:, :, half::2], diff[:, :, :],
                                            total[:, :].rearrange("p (t o) -> p t o", o=1)
                                            .to_broadcast([TT, NTT, N_EXP1]), ALU.mult))
        nc.all_engine_barrier()
        experts(st, "1", hT, comb, resid, N_ALL1, F1, t["gu1"], t["dn1"])
    nc.all_engine_barrier()
    fetched(sp, sp.dma_start(token_tiles(t["out"]), resid[:, :, :]))
    ctx.close()


def kernel(**inputs):
    import numpy as np
    import concourse.bacc as bacc
    from concourse.bass_utils import run_bass_kernel_spmd as run

    a = {k: np.asarray(v) for k, v in inputs.items()}

    def gate_up(g, u):
        both = np.concatenate([g, u], axis=2)
        n, _, w = both.shape
        return both.reshape(n, NC, P, w).transpose(0, 2, 1, 3).reshape(n, P, NC * w)

    sg = a["L0_ffn_sg"].reshape(DIM, 2, F0).transpose(1, 0, 2)
    su = a["L0_ffn_su"].reshape(DIM, 2, F0).transpose(1, 0, 2)
    sd = a["L0_ffn_sd"].reshape(2, F0, DIM)
    w1 = a["L1_ffn_w1"].transpose(0, 2, 1).reshape(N_EXP1, DIM, 2, 2, F1)
    w1 = w1.transpose(2, 0, 3, 1, 4).reshape(2, N_ALL1, DIM, F1)
    w2 = a["L1_ffn_w2"].transpose(0, 2, 1).reshape(N_ALL1, F1, DIM)
    arrays = {
        "x": a["x"].reshape(TOK, DIM),
        "ctxT": a["ctx_2048"].reshape(NKEY, DIM).T,
        "gu0": gate_up(np.concatenate([a["L0_ffn_wg"], sg]), np.concatenate([a["L0_ffn_wu"], su])),
        "dn0": np.concatenate([a["L0_ffn_wd"], sd]),
        "gu1": gate_up(w1[0], w1[1]),
        "dn1": w2,
        "W_inT": a["L1_xattn_W_in"].T,
        "W_outT": a["L1_xattn_W_out"].T,
        "router_wT": a["L1_ffn_router_w"].T,
        "L1_xattn_decay": a["L1_xattn_decay"].reshape(1),
    }
    for n in ("L0_xattn_Wq", "L0_xattn_bq", "L0_xattn_Wkv", "L0_xattn_bkv", "L0_xattn_Wp", "L0_xattn_bp",
              "L0_ffn_gate_w", "L1_xattn_b_in", "L1_xattn_b_out", "L1_xattn_gamma", "L1_xattn_beta"):
        arrays[n] = a[n]
    arrays = {n: np.ascontiguousarray(v) for n, v in arrays.items()}

    nc = bacc.Bacc("TRN2", target_bir_lowering=False, num_devices=1)
    f32 = mybir.dt.float32
    t = {n: nc.dram_tensor("in_" + n, v.shape, f32, kind="ExternalInput").ap() for n, v in arrays.items()}
    t["out"] = nc.dram_tensor("out_0", (TOK, DIM), f32, kind="ExternalOutput").ap()
    build(nc, t)
    res = run(nc, [{"in_" + n: v for n, v in arrays.items()}], core_ids=[0])
    return np.asarray(res.results[0]["out_0"]).reshape(BATCH, SEQ, DIM)
```
